# Optimizing a Trainium2 kernel written in Bass

```python
import numpy as np
import jax
import jax.numpy as jnp

def _softmax(x, axis=-1):
    return jax.nn.softmax(x, axis=axis)

def _gelu(x):
    return jax.nn.gelu(x, approximate=True)

def _silu(x):
    return jax.nn.silu(x)

def _sigmoid(x):
    return jax.nn.sigmoid(x)

def _layernorm(x, axis=-1, eps=1e-05):
    m = jnp.mean(x, axis=axis, keepdims=True)
    v = jnp.var(x, axis=axis, keepdims=True)
    return (x - m) / jnp.sqrt(v + eps)

def _scatter_add(tgt, idx, src, axis=0):
    return tgt.at[idx].add(src)

def _segment_sum(src, seg, n):
    return jax.ops.segment_sum(src, seg, n)
kernel_name = 'mk_gnn_preln_d1_gnn_r32_a4e86e'

def setup_inputs(seed: int=0):
    np.random.seed(seed)
    _w = jnp.asarray

    def _rec_inputs():
        import jax
        import jax.numpy as jnp
        _gk = jax.random.key(seed)
        x = -0.0005121 + 1.001 * jax.random.normal(jax.random.fold_in(_gk, 1), (3125, 32), jnp.float32)
        _s = jax.random.randint(jax.random.fold_in(_gk, 2), (50000,), 0, 3125, jnp.int32)
        _d = jax.random.randint(jax.random.fold_in(_gk, 3), (50000,), 0, 3125, jnp.int32)
        _loop = jnp.arange(3125, dtype=jnp.int32)
        src = jnp.concatenate([_s, _d, _loop])
        dst = jnp.concatenate([_d, _s, _loop])
        _o = jnp.argsort(dst, stable=True)
        src = src[_o]
        dst = dst[_o]
        edge_attr_32 = -5.3897e-05 + 0.999841 * jax.random.normal(jax.random.fold_in(_gk, 12), (103125, 32), jnp.float32)
        return (x, src, dst, edge_attr_32)
    x, src, dst, edge_attr_32 = _rec_inputs()

    def _L0_gnn_setup():
        import jax, jax.numpy as jnp
        import numpy as np
        N = 3125
        E = 25000
        H = 4
        D = 32
        NL = 3
        DN = 32
        DE = 32

        def _egat_layer(nf, ef, src, dst, W_ni, W_nj, W_fij, W_node, attn, bias):
            f_ni = nf @ W_ni
            f_nj = nf @ W_nj
            f_fij = ef @ W_fij
            f_out = f_ni[src] + f_nj[dst] + f_fij + bias
            f_out = jax.nn.leaky_relu(f_out, 0.2).reshape(-1, H, D)
            e = jnp.einsum('ehd,hd->eh', f_out, attn)
            emax = jax.ops.segment_max(e, dst, num_segments=N)
            a = jnp.exp(e - emax[dst])
            denom = jax.ops.segment_sum(a, dst, num_segments=N)
            a = a / denom[dst]
            h = (nf @ W_node).reshape(-1, H, D)
            m = h[src] * a[:, :, None]
            h_out = jax.ops.segment_sum(m, dst, num_segments=N)
            return (h_out, f_out)
        key = jax.random.key(seed)
        ks = jax.random.split(key, 10)
        s = 1.0 / np.sqrt(DN)
        inp = {'nf': jax.random.normal(ks[0], (N, DN), jnp.float32), 'ef': jax.random.normal(ks[1], (E, DE), jnp.float32), 'src': jax.random.randint(ks[2], (E,), 0, N, jnp.int32), 'dst': jax.random.randint(ks[3], (E,), 0, N, jnp.int32), 'W_ni': jax.random.normal(ks[4], (NL, DN, H * D), jnp.float32) * s, 'W_nj': jax.random.normal(ks[5], (NL, DN, H * D), jnp.float32) * s, 'W_fij': jax.random.normal(ks[6], (NL, DE, H * D), jnp.float32) * s, 'W_node': jax.random.normal(ks[7], (NL, DN, H * D), jnp.float32) * s, 'attn': jax.random.normal(ks[8], (NL, H, D), jnp.float32) * s, 'bias': jnp.zeros((NL, H * D), jnp.float32)}
        return inp
    _L0_gnn_all = _L0_gnn_setup()
    _L0_gnn_in = {k: v for k, v in _L0_gnn_all.items() if k in ('W_ni', 'W_nj', 'W_fij', 'W_node', 'attn', 'bias')}
    del _L0_gnn_all
    return {'x': x, 'src': src, 'dst': dst, 'edge_attr_32': edge_attr_32, 'L0_gnn_W_ni': _L0_gnn_in['W_ni'], 'L0_gnn_W_nj': _L0_gnn_in['W_nj'], 'L0_gnn_W_fij': _L0_gnn_in['W_fij'], 'L0_gnn_W_node': _L0_gnn_in['W_node'], 'L0_gnn_attn': _L0_gnn_in['attn'], 'L0_gnn_bias': _L0_gnn_in['bias']}

def reference(x, src, dst, edge_attr_32, L0_gnn_W_ni, L0_gnn_W_nj, L0_gnn_W_fij, L0_gnn_W_node, L0_gnn_attn, L0_gnn_bias):
    import jax
    import jax.numpy as jnp

    def _L0_gnn_ref(nf, ef, src, dst, W_ni, W_nj, W_fij, W_node, attn, bias):
        import jax, jax.numpy as jnp
        import numpy as np
        N = 3125
        E = 25000
        H = 4
        D = 32
        NL = 3
        DN = 32
        DE = 32

        def _egat_layer(nf, ef, src, dst, W_ni, W_nj, W_fij, W_node, attn, bias):
            f_ni = nf @ W_ni
            f_nj = nf @ W_nj
            f_fij = ef @ W_fij
            f_out = f_ni[src] + f_nj[dst] + f_fij + bias
            f_out = jax.nn.leaky_relu(f_out, 0.2).reshape(-1, H, D)
            e = jnp.einsum('ehd,hd->eh', f_out, attn)
            emax = jax.ops.segment_max(e, dst, num_segments=N)
            a = jnp.exp(e - emax[dst])
            denom = jax.ops.segment_sum(a, dst, num_segments=N)
            a = a / denom[dst]
            h = (nf @ W_node).reshape(-1, H, D)
            m = h[src] * a[:, :, None]
            h_out = jax.ops.segment_sum(m, dst, num_segments=N)
            return (h_out, f_out)
        for l in range(NL):
            nfh, efh = _egat_layer(nf, ef, src, dst, W_ni[l], W_nj[l], W_fij[l], W_node[l], attn[l], bias[l])
            nf = nfh.mean(axis=1)
            ef = efh.mean(axis=1)
        return nf
    h = jnp.maximum(_layernorm(x, axis=-1), 0.0)
    x = x + _L0_gnn_ref(h, edge_attr_32, src, dst, L0_gnn_W_ni, L0_gnn_W_nj, L0_gnn_W_fij, L0_gnn_W_node, L0_gnn_attn, L0_gnn_bias)
    return x

_drawn_inputs = setup_inputs


def setup_inputs(seed=0):
    import zlib

    import numpy as np

    out = dict(_drawn_inputs(seed))
    spreads = {'L0_gnn_bias': (0.0, 0.8)}
    factors = {'edge_attr_32': 8.0,
     'L0_gnn_W_ni': 8.0,
     'L0_gnn_W_nj': 8.0,
     'L0_gnn_W_fij': 8.0,
     'L0_gnn_attn': 8.0}
    for name, (base, spread) in spreads.items():
        noise = np.random.default_rng([zlib.crc32(name.encode()), seed]).standard_normal(out[name].shape)
        drawn = base * np.exp(spread * noise) if base else spread * noise
        out[name] = jnp.asarray(drawn.astype(out[name].dtype))
    for name, factor in factors.items():
        out[name] = (out[name] * factor).astype(out[name].dtype)
    return out
```

```python
from contextlib import ExitStack

import concourse.bass as bass
from concourse import mybir

F32 = mybir.dt.float32
I32 = mybir.dt.int32
ALU = mybir.AluOpType
ACT = mybir.ActivationFunctionType
AX = mybir.AxisListType

P = 128
TB = 68
GT = 4
BIG = 1e38
FAR = float(1 << 20)


def egat_kernel(nc, x, src, dst, edge_attr, W_ni, W_nj, W_fij, W_node, attn, bias, out):
    N, D = x.shape
    E = src.shape[0]
    L, H, _ = attn.shape
    HD = H * D
    C = D + 1
    HC = H * C
    K = C + 2 * D
    DST0, EF0 = C, C + D
    NB = -(-E // (P * TB))
    NB += NB % 2
    T = NB * TB
    NP = NB // 2
    NG = TB // GT
    FULL = E // T
    REST = E - FULL * T
    NQ = 125
    NCOL = N // NQ
    M = H + D
    assert NQ * NCOL == N and TB % GT == 0 and HD == P and FULL < P and E < P * T
    SLOPE = 0.2
    PAD = P * T - E
    PADR = 98
    assert PAD * D % PADR == 0 and PAD * D // PADR <= TB * HC

    nf_tab = nc.dram_tensor("nf_tab", (N, C), F32, kind="Internal").ap()
    ef_tab = nc.dram_tensor("ef_tab", (P * T, D), F32, kind="Internal").ap()
    edge_first = nc.dram_tensor("edge_first", (P * T, D), F32, kind="Internal").ap()
    u_tab = nc.dram_tensor("u_tab", (P * T, HC), F32, kind="Internal").ap()
    m_tab = nc.dram_tensor("m_tab", (P * T, H), F32, kind="Internal").ap()
    dst_tab = nc.dram_tensor("dst_tab", (P, T), F32, kind="Internal").ap()
    run_tab = nc.dram_tensor("run_tab", (N + 1, 1), F32, kind="Internal").ap()

    ef_blk = ef_tab.rearrange("(p t) d -> p (t d)", t=T)
    first_blk = edge_first.rearrange("(p t) d -> p (t d)", t=T)
    u_blk = u_tab.rearrange("(p t) c -> p (t c)", t=T)
    m_blk = m_tab.rearrange("(p t) h -> p (t h)", t=T)

    with ExitStack() as ctx:
        def sb(name, shape, dt=F32):
            return ctx.enter_context(nc.sbuf_tensor(name, shape, dt))

        def ps(name, shape):
            return ctx.enter_context(nc.psum_tensor(name, shape, F32))

        def sem(name):
            return ctx.enter_context(nc.semaphore(name))

        rows = [sb(f"rows{s}", [P, TB * K]) for s in range(2)]
        rows3 = [r[:, :].rearrange("p (t k) -> p t k", k=K) for r in rows]
        first_st = sb("first_st", [P, TB * D])
        ef_st = sb("ef_st", [P, TB * D])
        ef_new = [sb(f"ef_new{s}", [P, TB * D]) for s in range(2)]
        U = [sb(f"U{s}", [P, TB * HC]) for s in range(2)]
        U3 = [u[:, :].rearrange("p (t c) -> p t c", c=HC) for u in U]
        sc = [sb(f"sc{s}", [P, TB * H]) for s in range(2)]
        mx = [sb(f"mx{s}", [P, (TB + 1) * H]) for s in range(2)]
        expo = sb("expo", [P, 2, TB * H])
        wts = sb("wts", [P, 2, TB * H])
        same_b = [sb(f"same_b{s}", [P, TB]) for s in range(2)]
        cut_b = [sb(f"cut_b{s}", [P, TB]) for s in range(2)]
        idx = [sb(f"idx{s}", [P, TB], I32) for s in range(2)]
        xT = [sb(f"xT{s}", [P, GT * P]) for s in range(2)]
        lr = [sb(f"lr{s}", [P, GT * P]) for s in range(2)]
        src_sb = sb("src_sb", [P, T], I32)
        same = sb("same", [P, T])
        cut = sb("cut", [P, T])
        ident = sb("ident", [P, P])
        nf = sb("nf", [NQ, NCOL * C])
        nf3 = nf[:, :].rearrange("q (b c) -> q b c", c=C)
        x_sb = sb("x_sb", [NQ, NCOL * D])
        w_edge = sb("w_edge", [K, HD])
        w_out = sb("w_out", [P, M])
        w_turn = sb("w_turn", [HD, K])
        w_mix = sb("w_mix", [K, M])
        w_node = sb("w_node", [P, D])
        w_mean = sb("w_mean", [P, D])
        first_idx = sb("first_idx", [NQ, NCOL], I32)
        last_idx = sb("last_idx", [NQ, NCOL], I32)
        has_edge = sb("has_edge", [NQ, NCOL])
        d1_idx = sb("d1_idx", [P, 1], I32)
        joined = sb("joined", [P, P])
        apart = sb("apart", [P, P])
        end_get = sb("end_get", [P, 1], I32)
        end_put = sb("end_put", [P, 1], I32)
        nf_d1 = sb("nf_d1", [P, C])
        m_spread = sb("m_spread", [P, H * P])
        jw = sb("jw", [P, H * P])
        jwT = sb("jwT", [P, H * P])
        m_in = sb("m_in", [P, H])
        m_end = sb("m_end", [P, H])
        m_all = sb("m_all", [P, H])
        j_exp = sb("j_exp", [P, 2, H])
        j_wts = sb("j_wts", [P, 2, H])
        u_end = sb("u_end", [P, HC])
        u_in = sb("u_in", [P, HC])
        rden = sb("rden", [NQ, NCOL * H])

        xT_ps = [ps(f"xT_ps{s}", [P, GT * P]) for s in range(2)]
        f_ps = [ps(f"f_ps{s}", [P, GT * P]) for s in range(2)]
        o_ps = [ps(f"o_ps{s}", [P, GT * P]) for s in range(2)]
        n_ps = ps("n_ps", [P, 2 * GT * P])

        z4 = U[0][0:NQ, 0:NCOL * HC].rearrange("q (b h c) -> q b h c", h=H, c=C)
        s4 = U[1][0:NQ, 0:NCOL * HD].rearrange("q (b h d) -> q b h d", h=H, d=D)

        dcol = U[0][:, 0:T + 1].bitcast(I32)
        dcolf = U[1][:, 0:T + 1]
        xmp = jw[:, 0:P].bitcast(I32)
        first_f, next_f, node_f, part_f = (rden[:, a * NCOL:(a + 1) * NCOL] for a in range(4))
        mean = m_spread[0:NQ, 0:NCOL]
        var = m_spread[0:NQ, NCOL:2 * NCOL]
        xc = ef_new[0][0:NQ, 0:NCOL * D].rearrange("q (b d) -> q b d", d=D)
        xsq = ef_new[1][0:NQ, 0:NCOL * D].rearrange("q (b d) -> q b d", d=D)
        x3 = x_sb[:, :].rearrange("q (b d) -> q b d", d=D)
        first3 = first_st[:, :].rearrange("p (t d) -> p t d", d=D)
        sc3 = [a[:, :].rearrange("p (t h) -> p t h", h=H) for a in sc]
        mx3 = [a[:, :].rearrange("p (t h) -> p t h", h=H) for a in mx]

        zeroed = sem("zeroed")
        made = sem("made")
        dst_in = sem("dst_in")
        src_in = sem("src_in")
        x_in = sem("x_in")
        prep = sem("prep")
        lasts_t = sem("lasts_t")
        rooted = sem("rooted")
        dst_out = sem("dst_out")
        chunk_idx = sem("chunk_idx")
        chunk_in = [sem(f"chunk_in{s}") for s in range(2)]
        counted = sem("counted")
        run_out = sem("run_out")
        run_in = sem("run_in")
        run_end_in = sem("run_end_in")
        first_zero = sem("first_zero")
        nf_ready = sem("nf_ready")
        tab_out = sem("tab_out")
        w_in = sem("w_in")
        w_turned = sem("w_turned")
        w_turn_ready = sem("w_turn_ready")
        w_mixed = sem("w_mixed")
        w_mix_ready = sem("w_mix_ready")
        w_used = sem("w_used")
        first_out = sem("first_out")
        d1_in = sem("d1_in")
        idx_copied = sem("idx_copied")
        src_rows = [sem(f"src_rows{s}") for s in range(2)]
        ef_in = sem("ef_in")
        first_in = sem("first_in")
        ef_spread = sem("ef_spread")
        dst_spread = sem("dst_spread")
        turned = sem("turned")
        xT_ready = sem("xT_ready")
        f_ready = sem("f_ready")
        lr_ready = sem("lr_ready")
        o_ready = sem("o_ready")
        sc_ready = sem("sc_ready")
        ef_out = [sem(f"ef_out{s}") for s in range(2)]
        max_done = sem("max_done")
        expo_done = sem("expo_done")
        wts_ready = sem("wts_ready")
        prod_done = sem("prod_done")
        sums_done = sem("sums_done")
        u_out = [sem(f"u_out{s}") for s in range(2)]
        sliced = sem("sliced")
        normed = sem("normed")
        m_wide = sem("m_wide")
        m_turned = sem("m_turned")
        end_in = sem("end_in")
        j = sem("j")
        j_exp1 = sem("j_exp1")
        jw_turned = sem("jw_turned")
        u_in_ready = sem("u_in_ready")
        j_exp2 = sem("j_exp2")
        u_fixed = sem("u_fixed")
        z_in = sem("z_in")
        nd = sem("nd")
        s_turned = sem("s_turned")
        sT_ready = sem("sT_ready")
        n_ready = sem("n_ready")
        x_out = sem("x_out")

        passed = {e: sem(f"passed_{e}") for e in ("sp", "pool", "pe")}

        EFI = (16, 32)
        UI = (32, 16)
        DB = NQ
        groups = [range(g, min(g + GT, NCOL)) for g in range(0, NCOL, GT)]
        JS, NS = 11, 4
        WI = 16 * (4 + 2 * H)

        with nc.Block() as block:

            @block.sync
            def _(eng):
                eng.wait_ge(zeroed, 3)
                eng.dma_start(dcol[0:FULL, 1:T + 1],
                              dst[0:FULL * T].rearrange("(p t) -> p t", t=T)).then_inc(dst_in, 16)
                eng.dma_start(dcol[FULL:FULL + 1, 1:REST + 1],
                              dst[FULL * T:E].rearrange("(p t) -> p t", p=1)).then_inc(dst_in, 16)
                eng.dma_start(dcol[1:FULL + 1, 0:1],
                              dst[T - 1:FULL * T].rearrange("(p t) -> p t", t=1)[::T, :]
                              , allow_slow_non_contiguous=True).then_inc(dst_in, 16)
                eng.dma_start(src_sb[0:FULL, :],
                              src[0:FULL * T].rearrange("(p t) -> p t", t=T)).then_inc(src_in, 16)
                eng.dma_start(src_sb[FULL:FULL + 1, 0:REST],
                              src[FULL * T:E].rearrange("(p t) -> p t", p=1)).then_inc(src_in, 16)
                eng.dma_start(x_sb[:, :],
                              x.rearrange("(q b) d -> q (b d)", b=NCOL)).then_inc(x_in, 16)
                eng.wait_ge(prep, 1)
                eng.dma_start(dst_tab[:, :], U[1][:, 1:T + 1]).then_inc(dst_out, 16)
                eng.dma_start(ef_tab[0:FULL * T, :].rearrange("(p t) d -> p (t d)", t=T),
                              edge_attr[0:FULL * T, :].rearrange("(p t) d -> p (t d)", t=T)
                              ).then_inc(ef_out[0], 16)
                eng.dma_start(ef_tab[FULL * T:E, :], edge_attr[FULL * T:E, :]
                              ).then_inc(ef_out[1], 16)
                eng.wait_ge(prep, 12)
                eng.dma_start(run_tab[0:N, :].rearrange("(q b) o -> q (b o)", b=NCOL),
                              rden[:, 0:NCOL]).then_inc(run_out, 16)
                eng.dma_start(run_tab[N:N + 1, :], u_end[0:1, 0:1]).then_inc(run_out, 16)
                eng.wait_ge(run_out, 32)
                eng.dma_start(rden[:, NCOL:2 * NCOL],
                              run_tab[1:N + 1, :].rearrange("(q b) o -> q (b o)", b=NCOL)
                              ).then_inc(run_in, 16)
                eng.wait_ge(zeroed, 6)
                w = TB * HC
                eng.dma_start(first_blk[:, 0:w], U[0][:, :]).then_inc(u_out[0], 16)
                eng.dma_start(first_blk[:, w:2 * w], U[0][:, :]).then_inc(u_out[0], 16)
                eng.dma_start(first_blk[:, 2 * w:T * D], U[1][:, 0:T * D - 2 * w]
                              ).then_inc(u_out[1], 16)
                eng.dma_start(ef_tab[E:P * T, :].rearrange("a d -> (a d)")
                              .rearrange("(r w) -> r w", r=PADR),
                              U[1][0:PADR, 0:PAD * D // PADR]).then_inc(ef_out[1], 16)
                eng.wait_ge(u_out[0], UI[0])
                eng.wait_ge(u_out[1], UI[1])
                eng.wait_ge(ef_out[1], EFI[1])
                eng.sem_inc(first_zero, 1)

                with eng.Fori(0, L, 1) as l:
                    eng.wait_ge(w_used, l + 1)
                    eng.wait_ge(o_ready, l * (NB * NG) + 2)
                    eng.sem_inc(passed["sp"], 1)
                    lw = bass.ds(l, 1)

                    def one(ap):
                        return ap.rearrange("a b c -> (a b) c")
                    eng.dma_start(w_edge[0:D, :], one(W_ni[lw, :, :])).then_inc(w_in, 16)
                    eng.dma_start(w_edge[D:C, :], bias[lw, :]).then_inc(w_in, 16)
                    eng.dma_start(w_edge[DST0:EF0, :], one(W_nj[lw, :, :])).then_inc(w_in, 16)
                    eng.dma_start(w_edge[EF0:K, :], one(W_fij[lw, :, :])).then_inc(w_in, 16)
                    for h in range(H):
                        eng.dma_start(w_out[h * D:(h + 1) * D, h:h + 1],
                                      attn[lw, h, :].rearrange("a d -> d a"),
                                      allow_slow_non_contiguous=True).then_inc(w_in, 16)
                        eng.dma_start(w_node[h * D:(h + 1) * D, :],
                                      one(W_node[lw, :, h * D:(h + 1) * D])).then_inc(w_in, 16)
                    eng.wait_ge(nf_ready, l + 1)
                    eng.dma_start(nf_tab.rearrange("(q b) c -> q (b c)", b=NCOL), nf[:, :]
                                  ).then_inc(tab_out, 16)
                    eng.wait_ge(ef_out[0], l * (16 * NP) + EFI[0])
                    eng.sem_inc(passed["sp"], 1)
                    eng.wait_ge(ef_out[1], l * (16 * NP) + EFI[1])
                    eng.wait_ge(first_out, l * (16 * NCOL) + 16 * NCOL)
                    eng.sem_inc(passed["sp"], 1)

                    def load(k, col):
                        eng.wait_ge(ef_spread, k)
                        eng.dma_start(ef_st[:, :], ef_blk[:, bass.ds(col, TB * D)]
                                      ).then_inc(ef_in, 16)
                        eng.wait_ge(dst_spread, k * D)
                        eng.dma_start(first_st[:, :], first_blk[:, bass.ds(col, TB * D)]
                                      ).then_inc(first_in, 16)

                    def store(k, b):
                        s = k[1]
                        eng.wait_ge(sums_done, k[0] * HC + (l + (HC + 1)))
                        eng.dma_start(u_blk[:, bass.ds(b * (TB * HC), TB * HC)], U[s][:, :]
                                      ).then_inc(u_out[s], 16)
                        eng.dma_start(m_blk[:, bass.ds(b * (TB * H), TB * H)], mx[s][:, H:]
                                      ).then_inc(u_out[s], 16)

                    load(l * NB + 1, 0)
                    load(l * NB + 2, TB * D)
                    with eng.Fori(0, NP - 1, 1) as i:
                        for s in range(2):
                            k = l * NB + i * 2 + s
                            load(k + 3, (i * 2 + (s + 2)) * (TB * D))
                            store((k, s), i * 2 + s)
                    for s in range(2):
                        store((l * NB + (NB - 2 + s), s), NB - 2 + s)
                eng.wait_ge(nf_ready, L + 2)
                eng.dma_start(out.rearrange("(q b) d -> q (b d)", b=NCOL), x_sb[:, :]
                              ).then_inc(x_out, 16)
                eng.wait_ge(x_out, 16)
                eng.wait_ge(ef_out[0], EFI[0] + 16 * NP * L)
                eng.wait_ge(ef_out[1], EFI[1] + 16 * NP * L)

            @block.gpsimd
            def _(eng):
                eng.iota(jw[:, 0:P].bitcast(I32), pattern=[[1, P]], base=0, channel_multiplier=-1
                         ).then_inc(made, 1)
                eng.iota(first_idx[:, :], pattern=[[1, NCOL]], base=0, channel_multiplier=NCOL
                         ).then_inc(made, 1)
                eng.iota(end_get[:, :], pattern=[[0, 1]], base=0, channel_multiplier=T
                         ).then_inc(made, 1)
                eng.wait_ge(dst_out, 16)
                eng.wait_ge(chunk_idx, 1)
                for b in range(NCOL):
                    if b >= 2:
                        eng.wait_ge(counted, b - 1)
                    eng.indirect_dma_start(rows[b % 2][0:NQ, 0:T], None, dst_tab[:, :],
                                           bass.IndirectOffsetOnAxis(
                                               ap=last_idx[:, b:b + 1], axis=0)
                                           ).then_inc(chunk_in[b % 2], 16)
                eng.wait_ge(run_out, 32)
                eng.wait_ge(prep, 13)
                eng.indirect_dma_start(m_in[:, 0:1], None, run_tab[:, :],
                                       bass.IndirectOffsetOnAxis(ap=d1_idx[:, 0:1], axis=0)
                                       ).then_inc(run_end_in, 16)
                eng.wait_ge(prep, 30)
                eng.wait_ge(src_in, 32)
                eng.wait_ge(first_zero, 1)

                with eng.Fori(0, L, 1) as l:
                    eng.wait_ge(nf_ready, l + 1)
                    eng.sem_inc(passed["pool"], 1)
                    for b in range(NCOL):
                        eng.indirect_dma_start(edge_first[:, :],
                                               bass.IndirectOffsetOnAxis(
                                                   ap=first_idx[:, b:b + 1], axis=0),
                                               nf[:, b * C:b * C + D], None,
                                               bounds_check=P * T - 1, oob_is_err=False
                                               ).then_inc(first_out, 16)
                    eng.wait_ge(tab_out, l * 16 + 16)
                    eng.sem_inc(passed["pool"], 1)
                    eng.indirect_dma_start(nf_d1[:, :], None, nf_tab[:, :],
                                           bass.IndirectOffsetOnAxis(ap=d1_idx[:, 0:1], axis=0)
                                           ).then_inc(d1_in, 16)
                    with eng.Fori(0, NP, 1) as i:
                        for s in range(2):
                            k = l * NB + i * 2 + s
                            eng.wait_ge(turned, k * NG + NG)
                            eng.wait_ge(prod_done, k + 1)
                            eng.tensor_copy(idx[s][:, :],
                                            src_sb[:, bass.ds((i * 2 + s) * TB, TB)]
                                            ).then_inc(idx_copied, 1)
                            eng.wait_ge(idx_copied, k + 1)
                            eng.sem_inc(passed["pool"], 1)
                            for t in range(TB):
                                eng.indirect_dma_start(rows[s][:, t * K:t * K + C], None,
                                                       nf_tab[:, :],
                                                       bass.IndirectOffsetOnAxis(
                                                           ap=idx[s][:, t:t + 1], axis=0)
                                                       ).then_inc(src_rows[s], 16)
                    eng.wait_ge(u_out[0], l * (32 * NP) + (UI[0] + 32 * NP))
                    eng.wait_ge(u_out[1], l * (32 * NP) + (UI[1] + 32 * NP))
                    eng.sem_inc(passed["pool"], 1)
                    eng.indirect_dma_start(u_end[:, :], None, u_tab[:, :],
                                           bass.IndirectOffsetOnAxis(ap=end_get[:, 0:1], axis=0)
                                           ).then_inc(end_in, 16)
                    eng.indirect_dma_start(m_end[:, :], None, m_tab[:, :],
                                           bass.IndirectOffsetOnAxis(ap=end_get[:, 0:1], axis=0)
                                           ).then_inc(end_in, 16)
                    eng.wait_ge(j, l * JS + JS)
                    eng.sem_inc(passed["pool"], 1)
                    eng.indirect_dma_start(u_tab[:, :],
                                           bass.IndirectOffsetOnAxis(ap=end_put[:, 0:1], axis=0),
                                           u_end[:, :], None,
                                           bounds_check=P * T - 1, oob_is_err=False
                                           ).then_inc(u_fixed, 16)
                    eng.wait_ge(u_fixed, l * 16 + 16)
                    eng.sem_inc(passed["pool"], 1)
                    for b in range(NCOL):
                        eng.indirect_dma_start(U[0][0:NQ, b * HC:(b + 1) * HC], None,
                                               u_tab[:, :],
                                               bass.IndirectOffsetOnAxis(
                                                   ap=last_idx[:, b:b + 1], axis=0)
                                               ).then_inc(z_in, 16)

            @block.tensor
            def _(eng):
                eng.wait_ge(prep, 3)
                eng.transpose(f_ps[0][:, 0:P], jwT[:, 0:P], ident[:, :]).then_inc(lasts_t, 1)
                eng.sem_inc(turned, 2 * NG)
                eng.sem_inc(f_ready, 2)
                eng.sem_inc(o_ready, 2)

                with eng.Fori(0, L, 1) as l:
                    eng.wait_ge(w_in, l * WI + WI)
                    eng.sem_inc(passed["pe"], 1)
                    eng.wait_ge(nf_ready, l + 1)
                    eng.transpose(n_ps[:, 0:K], w_edge[:, :], ident[0:K, 0:K]
                                  ).then_inc(w_turned, 1)
                    eng.wait_ge(w_turn_ready, l + 1)
                    eng.matmul(n_ps[0:K, GT * P:GT * P + M], w_turn[:, :], w_out[:, :],
                               start=True, stop=True).then_inc(w_mixed, 1)
                    eng.wait_ge(w_mix_ready, l + 1)
                    eng.sem_inc(passed["pe"], 1)

                    def turn(k, s, g):
                        n, y = k * NG + g, (s * NG + g) % 2
                        eng.wait_ge(xT_ready, n + 1)
                        for u in range(GT):
                            t = g * GT + u
                            mm = eng.transpose(xT_ps[y][0:K, u * P:(u + 1) * P],
                                               rows3[s][:, t, :], ident[:, :])
                        mm.then_inc(turned, 1)

                    def edges(k, s, g):
                        n, y = k * NG + g, (s * NG + g) % 2
                        eng.wait_ge(xT_ready, n + 3)
                        eng.wait_ge(lr_ready, n + 1)
                        eng.wait_ge(sc_ready, n * 2 + 2)
                        for u in range(GT):
                            eng.matmul(o_ps[y][:, u * M:(u + 1) * M],
                                       xT[y][0:K, u * P:(u + 1) * P], w_mix[:, :],
                                       start=(u == 0), stop=False, skip_group_check=True)
                        eng.matmul(f_ps[y][:, :], w_edge[:, :], xT[y][0:K, :],
                                   start=True, stop=True).then_inc(f_ready, 1)

                    def scores(k, s, g):
                        n, y = k * NG + g, (s * NG + g) % 2
                        eng.wait_ge(lr_ready, n + 3)
                        for u in range(GT):
                            mm = eng.matmul(o_ps[y][:, u * M:(u + 1) * M],
                                            lr[y][:, u * P:(u + 1) * P], w_out[:, :],
                                            start=False, stop=(u == GT - 1),
                                            skip_group_check=True)
                        mm.then_inc(o_ready, 1)

                    with eng.Fori(0, NP, 1) as i:
                        for s in range(2):
                            k = l * NB + i * 2 + s
                            eng.wait_ge(src_rows[s], (l * NP + i) * (16 * TB) + 16 * TB)
                            eng.wait_ge(dst_spread, k * D + 2 * D)
                            eng.wait_ge(ef_spread, k + 2)
                            for g in range(NG + 2):
                                if g < NG:
                                    turn(k, s, g)
                                if 1 <= g <= NG:
                                    edges(k, s, g - 1)
                                if g >= 2:
                                    scores(k, s, g - 2)
                    eng.wait_ge(m_wide, l * H + H)
                    for h in range(H):
                        mm = eng.transpose(f_ps[0][:, h * P:(h + 1) * P],
                                           m_spread[:, h * P:(h + 1) * P], ident[:, :])
                    mm.then_inc(m_turned, 1)
                    eng.wait_ge(j, l * JS + 4)
                    for h in range(H):
                        mm = eng.transpose(f_ps[1][:, h * P:(h + 1) * P],
                                           jw[:, h * P:(h + 1) * P], ident[:, :])
                    mm.then_inc(jw_turned, 1)
                    eng.wait_ge(j, l * JS + 5)
                    for h in range(H):
                        mm = eng.matmul(o_ps[0][:, h * C:(h + 1) * C],
                                        jwT[:, h * P:(h + 1) * P],
                                        U3[1][:, TB - 1, h * C:(h + 1) * C],
                                        start=True, stop=True)
                    mm.then_inc(u_in_ready, 1)
                    eng.wait_ge(nd, l * NS + 3)

                    def node_turn(n):
                        if n >= 2:
                            eng.wait_ge(sT_ready, l * len(groups) + (n - 1))
                        for u, b in enumerate(groups[n]):
                            mm = eng.transpose(xT_ps[n % 2][:, u * DB:(u + 1) * DB],
                                               U[1][0:NQ, b * HD:(b + 1) * HD],
                                               ident[0:NQ, 0:NQ])
                        mm.then_inc(s_turned, 1)

                    node_turn(0)
                    for n in range(len(groups)):
                        if n + 1 < len(groups):
                            node_turn(n + 1)
                        eng.wait_ge(sT_ready, l * len(groups) + (n + 1))
                        for u, b in enumerate(groups[n]):
                            mm = eng.matmul(n_ps[0:NQ, b * D:(b + 1) * D],
                                            xT[n % 2][:, u * DB:(u + 1) * DB], w_mean[:, :],
                                            start=True, stop=True)
                        mm.then_inc(n_ready, 1)

            @block.scalar
            def _(eng):
                eng.sem_inc(xT_ready, 2)
                eng.sem_inc(lr_ready, 2)
                eng.sem_inc(sc_ready, 4)
                eng.sem_inc(ef_spread, 1)
                eng.wait_ge(normed, 5)
                eng.activation(var, var, ACT.Sqrt).then_inc(rooted, 1)

                with eng.Fori(0, L, 1) as l:
                    def spread(k, s):
                        eng.wait_ge(ef_in, k * 16 + 16)
                        eng.wait_ge(turned, k * NG + NG)
                        eng.activation(rows3[s][:, :, EF0:K],
                                       ef_st[:, :].rearrange("p (t d) -> p t d", d=D),
                                       ACT.Copy).then_inc(ef_spread, 1)

                    def take_xT(k, s, g):
                        n, y = k * NG + g, (s * NG + g) % 2
                        eng.wait_ge(turned, n + 2 * NG + 1)
                        eng.wait_ge(f_ready, n + 1)
                        eng.activation(xT[y][0:K, :], xT_ps[y][0:K, :], ACT.Copy
                                       ).then_inc(xT_ready, 1)

                    def leaky(k, s, g):
                        n, y = k * NG + g, (s * NG + g) % 2
                        eng.wait_ge(f_ready, n + 3)
                        eng.wait_ge(o_ready, n + 1)
                        eng.activation(lr[y][:, :], f_ps[y][:, :], ACT.Relu, scale=1 - SLOPE
                                       ).then_inc(lr_ready, 1)

                    def take_scores(k, s, g):
                        n, y = k * NG + g, (s * NG + g) % 2
                        eng.wait_ge(o_ready, n + 3)
                        o3 = o_ps[y][:, 0:GT * M].rearrange("p (t m) -> p t m", m=M)
                        eng.activation(sc[s][:, g * GT * H:(g + 1) * GT * H]
                                       .rearrange("p (t h) -> p t h", h=H),
                                       o3[:, :, 0:H], ACT.Copy).then_inc(sc_ready, 1)
                        eng.activation(ef_new[s][:, g * GT * D:(g + 1) * GT * D]
                                       .rearrange("p (t d) -> p t d", d=D),
                                       o3[:, :, H:M], ACT.Copy).then_inc(sc_ready, 1)

                    def block_steps(i, s, last):
                        k = l * NB + i * 2 + s
                        eng.wait_ge(prod_done, k + 1)
                        eng.wait_ge(ef_out[s], (l * NP + i) * 16 + EFI[s])
                        for g in range(NG + 2):
                            if g < NG:
                                take_xT(k, s, g)
                            if 1 <= g <= NG:
                                leaky(k, s, g - 1)
                            if g >= 2:
                                take_scores(k, s, g - 2)
                        eng.wait_ge(sc_ready, k * (2 * NG) + (2 * NG + 4))
                        eng.dma_start(ef_blk[:, bass.ds((i * 2 + s) * (TB * D), TB * D)],
                                      ef_new[s][:, :]).then_inc(ef_out[s], 16)
                        if not last:
                            spread(k + 1, 1 - s)
                        eng.wait_ge(expo_done, k * 3 + 3)
                        eng.activation(wts[:, :, :], expo[:, :, :], ACT.Exp).then_inc(wts_ready, 1)

                    spread(l * NB, 0)
                    with eng.Fori(0, NP - 1, 1) as i:
                        for s in range(2):
                            block_steps(i, s, False)
                    block_steps(NP - 1, 0, False)
                    block_steps(NP - 1, 1, True)

                    eng.wait_ge(j, l * JS + 3)
                    eng.activation(jw[:, :], jw[:, :], ACT.Exp).then_inc(j_exp1, 1)
                    eng.wait_ge(j, l * JS + 8)
                    eng.activation(j_wts[:, :, :], j_exp[:, :, :], ACT.Exp).then_inc(j_exp2, 1)
                    for n in range(len(groups)):
                        w = len(groups[n]) * DB
                        eng.wait_ge(s_turned, l * len(groups) + (n + 1))
                        if n >= 2:
                            eng.wait_ge(n_ready, l * len(groups) + (n - 1))
                        eng.activation(xT[n % 2][:, 0:w], xT_ps[n % 2][:, 0:w], ACT.Copy
                                       ).then_inc(sT_ready, 1)

            @block.vector
            def _(eng):
                def wide(ap, shape):
                    return ap.broadcast_to(shape)

                eng.memset(dcol, N).then_inc(zeroed, 1)
                eng.memset(src_sb[:, :], 0).then_inc(zeroed, 1)
                eng.wait_ge(zeroed, 2)
                eng.memset(dcol[0:1, 0:1], -1).then_inc(zeroed, 1)
                eng.memset(u_end[:, :], float(E)).then_inc(zeroed, 1)
                eng.sem_inc(prod_done, 2)
                eng.sem_inc(dst_spread, D)
                eng.wait_ge(dst_in, 48)
                eng.tensor_copy(dcolf, dcol).then_inc(prep, 1)
                eng.wait_ge(made, 3)
                eng.tensor_scalar(ident[:, :], xmp, 0.0, None, ALU.is_equal).then_inc(prep, 1)
                eng.wait_ge(prep, 1)
                eng.tensor_copy(jwT[:, 0:P], wide(dcolf[:, T:T + 1], [P, P])).then_inc(prep, 1)
                eng.tensor_tensor(same[:, :], dcolf[:, 1:T + 1], dcolf[:, 0:T], ALU.is_equal
                                  ).then_inc(prep, 1)
                eng.wait_ge(prep, 4)
                eng.tensor_scalar(cut[:, :], same[:, :], -1.0, BIG, ALU.add, ALU.mult
                                  ).then_inc(prep, 1)
                eng.tensor_copy(node_f, first_idx[:, :]).then_inc(prep, 1)
                eng.wait_ge(prep, 6)
                eng.wait_ge(lasts_t, 1)
                below = U[0][0:NQ, 0:NCOL * P].rearrange("q (b p) -> q b p", p=P)
                eng.tensor_tensor(below,
                                  wide(f_ps[0][0:NQ, 0:P].rearrange("q (o p) -> q o p", o=1),
                                       [NQ, NCOL, P]),
                                  wide(node_f.rearrange("q (b o) -> q b o", o=1), [NQ, NCOL, P]),
                                  ALU.is_lt).then_inc(prep, 1)
                eng.wait_ge(prep, 7)
                eng.tensor_reduce(part_f, below, AX.X, ALU.add).then_inc(prep, 1)
                eng.wait_ge(prep, 8)
                eng.tensor_copy(last_idx[:, :], part_f).then_inc(chunk_idx, 1)
                eng.tensor_scalar(jwT[:, P:2 * P], xmp, 0.0, None, ALU.is_lt).then_inc(prep, 1)
                eng.wait_ge(prep, 9)
                eng.scalar_tensor_tensor(joined[:, :], f_ps[0][:, 0:P], dcolf[:, 1:2],
                                         jwT[:, P:2 * P], ALU.is_equal, ALU.mult
                                         ).then_inc(prep, 1)
                eng.wait_ge(prep, 10)
                eng.tensor_scalar(apart[:, :], joined[:, :], -1.0, BIG, ALU.add, ALU.mult
                                  ).then_inc(prep, 1)
                for b in range(NCOL):
                    eng.wait_ge(chunk_in[b % 2], 16 * (b // 2 + 1))
                    eng.tensor_scalar(U[0][0:NQ, (b % 2) * T:(b % 2 + 1) * T],
                                      rows[b % 2][0:NQ, 0:T], node_f[:, b:b + 1], None,
                                      ALU.is_lt, ALU.add, accum_out=first_f[:, b:b + 1]
                                      ).then_inc(counted, 1)
                eng.wait_ge(counted, NCOL)
                eng.scalar_tensor_tensor(first_f, part_f, float(T), first_f, ALU.mult, ALU.add
                                         ).then_inc(prep, 1)
                eng.tensor_scalar(d1_idx[:, :], dcolf[:, 1:2], 1.0, float(N), ALU.add, ALU.min
                                  ).then_inc(prep, 1)
                eng.wait_ge(dst_out, 16)
                eng.tensor_copy(m_in[:, 1:2], end_get[:, :]).then_inc(prep, 1)
                eng.tensor_scalar(m_in[:, 2:3], dcolf[:, 1:2], float(N - 1), None, ALU.min
                                  ).then_inc(prep, 1)
                eng.wait_ge(prep, 15)
                eng.memset(U[0][:, :], 0.0).then_inc(zeroed, 1)
                eng.memset(U[1][:, :], 0.0).then_inc(zeroed, 1)
                eng.wait_ge(x_in, 16)
                wide_q = [NQ, NCOL, D]
                eng.tensor_reduce(mean, x3, AX.X, ALU.add).then_inc(normed, 1)
                eng.wait_ge(normed, 1)
                eng.tensor_scalar(mean, mean, 1.0 / D, None, ALU.mult).then_inc(normed, 1)
                eng.wait_ge(normed, 2)
                mean_w = wide(mean.rearrange("q (b o) -> q b o", o=1), wide_q)
                var_w = wide(var.rearrange("q (b o) -> q b o", o=1), wide_q)
                eng.tensor_tensor(xc, x3, mean_w, ALU.subtract).then_inc(normed, 1)
                eng.wait_ge(normed, 3)
                eng.tensor_tensor(xsq, xc, xc, ALU.mult).then_inc(normed, 1)
                eng.wait_ge(normed, 4)
                eng.tensor_reduce(var, xsq, AX.X, ALU.add).then_inc(prep, 1)
                eng.wait_ge(prep, 16)
                eng.tensor_scalar(var, var, 1.0 / D, 1e-5, ALU.mult, ALU.add).then_inc(normed, 1)
                eng.wait_ge(rooted, 1)
                eng.reciprocal(var, var).then_inc(normed, 1)
                eng.wait_ge(normed, 6)
                eng.tensor_tensor(xc, xc, var_w, ALU.mult).then_inc(normed, 1)
                eng.wait_ge(normed, 7)
                eng.memset(nf3[:, :, D:C], 1.0)
                eng.tensor_scalar(nf3[:, :, 0:D], xc, 0.0, None, ALU.max).then_inc(nf_ready, 1)
                eng.memset(w_out[:, :], 0.0).then_inc(prep, 1)
                eng.wait_ge(prep, 17)
                eng.tensor_reduce(w_out[:, H:M], ident[:, :].rearrange("p (h d) -> p d h", d=D),
                                  AX.X, ALU.add).then_inc(prep, 1)
                eng.wait_ge(prep, 18)
                eng.tensor_scalar(w_out[:, H:M], w_out[:, H:M], 1.0 / H, None, ALU.mult
                                  ).then_inc(w_used, 1)
                eng.wait_ge(run_in, 16)
                eng.wait_ge(run_end_in, 16)
                eng.tensor_tensor(has_edge[:, :], first_f, next_f, ALU.is_lt).then_inc(prep, 1)
                eng.wait_ge(prep, 19)
                eng.scalar_tensor_tensor(last_idx[:, :], next_f, -1.0, has_edge[:, :],
                                         ALU.add, ALU.mult).then_inc(prep, 1)
                eng.tensor_scalar(part_f, has_edge[:, :], -FAR, FAR, ALU.mult, ALU.add
                                  ).then_inc(prep, 1)
                eng.wait_ge(prep, 21)
                eng.tensor_tensor(first_idx[:, :], part_f, first_f, ALU.add).then_inc(prep, 1)
                col, here = m_end[:, 0:1], m_end[:, 1:2]
                eng.scalar_tensor_tensor(col, m_in[:, 0:1], -1.0, m_in[:, 1:2],
                                         ALU.add, ALU.subtract).then_inc(prep, 1)
                eng.wait_ge(prep, 23)
                eng.tensor_scalar(here, col, 0.0, None, ALU.is_ge).then_inc(prep, 1)
                eng.wait_ge(prep, 24)
                eng.scalar_tensor_tensor(here, col, float(T), here, ALU.is_lt, ALU.mult
                                         ).then_inc(prep, 1)
                eng.wait_ge(prep, 25)
                eng.tensor_tensor(m_end[:, 2:3], col, here, ALU.mult).then_inc(prep, 1)
                eng.tensor_scalar(m_end[:, 3:4], here, -FAR, FAR, ALU.mult, ALU.add
                                  ).then_inc(prep, 1)
                eng.wait_ge(prep, 27)
                eng.tensor_tensor(end_get[:, :], m_in[:, 1:2], m_end[:, 2:3], ALU.add
                                  ).then_inc(prep, 1)
                eng.scalar_tensor_tensor(end_put[:, :], m_in[:, 0:1], -1.0, m_end[:, 3:4],
                                         ALU.add, ALU.add).then_inc(prep, 1)
                eng.tensor_copy(d1_idx[:, :], m_in[:, 2:3]).then_inc(prep, 1)
                eng.wait_ge(prep, 30)

                with eng.Fori(0, L, 1) as l:
                    eng.wait_ge(w_in, l * WI + WI)
                    eng.tensor_scalar(w_mean[:, :], w_node[:, :], 1.0 / H, None, ALU.mult
                                      ).then_inc(w_used, 1)
                    eng.wait_ge(w_turned, l + 1)
                    eng.tensor_copy(w_turn[:, :], n_ps[:, 0:K]).then_inc(w_turn_ready, 1)
                    eng.wait_ge(w_mixed, l + 1)
                    eng.tensor_scalar(w_mix[:, :], n_ps[0:K, GT * P:GT * P + M], SLOPE, None,
                                      ALU.mult).then_inc(w_mix_ready, 1)
                    eng.memset(U3[1][:, TB - 1, :], 0.0).then_inc(sums_done, 1)
                    eng.memset(mx3[1][:, TB, :], -BIG).then_inc(max_done, 1)

                    def slice_b(k, col, s):
                        eng.tensor_copy(same_b[s][:, :], same[:, bass.ds(col, TB)]
                                        ).then_inc(sliced, 1)
                        eng.tensor_copy(cut_b[s][:, :], cut[:, bass.ds(col, TB)]
                                        ).then_inc(sliced, 1)

                    def spread_dst(k, s, first):
                        eng.wait_ge(first_in, k * 16 + 16)
                        eng.wait_ge(turned, k * NG + NG)
                        eng.wait_ge(sliced, k * 2 + 2)
                        eng.wait_ge(dst_spread, k * D + D)
                        for d in range(D):
                            before = (nf_d1[:, d:d + 1] if first
                                      else rows3[1 - s][:, TB - 1, DST0 + d:DST0 + d + 1])
                            eng.tensor_tensor_scan(rows3[s][:, :, DST0 + d], same_b[s][:, :],
                                                   first3[:, :, d], before,
                                                   ALU.mult, ALU.add).then_inc(dst_spread, 1)

                    def recur(k, i, s):
                        eng.wait_ge(sc_ready, k * (2 * NG) + (2 * NG + 4))
                        eng.wait_ge(u_out[s], (l * NP + i) * 32 + UI[s])
                        eng.wait_ge(max_done, k * (H + 1) + (l + 1))
                        eng.tensor_copy(mx3[s][:, 0, :], mx3[1 - s][:, TB, :]
                                        ).then_inc(max_done, 1)
                        for h in range(H):
                            eng.tensor_tensor_scan(mx3[s][:, 1:TB + 1, h], cut_b[s][:, :],
                                                   sc3[s][:, :, h], mx3[1 - s][:, TB, h:h + 1],
                                                   ALU.add, ALU.max).then_inc(max_done, 1)
                        eng.wait_ge(max_done, k * (H + 1) + (l + (H + 2)))
                        ex = [expo[:, a, :].rearrange("p (t h) -> p t h", h=H) for a in range(2)]
                        eng.tensor_tensor(ex[0], mx3[s][:, 0:TB, :], mx3[s][:, 1:TB + 1, :],
                                          ALU.subtract).then_inc(expo_done, 1)
                        eng.tensor_tensor(ex[1], sc3[s], mx3[s][:, 1:TB + 1, :],
                                          ALU.subtract).then_inc(expo_done, 1)
                        eng.wait_ge(expo_done, k * 3 + 2)
                        eng.tensor_tensor(ex[0], ex[0],
                                          wide(cut_b[s][:, :].rearrange("p (t o) -> p t o", o=1),
                                               [P, TB, H]), ALU.add).then_inc(expo_done, 1)
                        eng.wait_ge(wts_ready, k + 1)
                        full = [P, TB, H, C]
                        eng.tensor_tensor(
                            U[s][:, :].rearrange("p (t h c) -> p t h c", h=H, c=C),
                            wide(rows3[s][:, :, 0:C].rearrange("p t (o c) -> p t o c", o=1), full),
                            wide(wts[:, 1, :].rearrange("p (t h o) -> p t h o", h=H, o=1), full),
                            ALU.mult).then_inc(prod_done, 1)
                        eng.wait_ge(prod_done, k + 3)
                        eng.wait_ge(sums_done, k * HC + (l + 1))
                        decay = wts[:, 0, :].rearrange("p (t h) -> p t h", h=H)
                        for c in range(HC):
                            eng.tensor_tensor_scan(U3[s][:, :, c], decay[:, :, c // C],
                                                   U3[s][:, :, c], U3[1 - s][:, TB - 1, c:c + 1],
                                                   ALU.mult, ALU.add).then_inc(sums_done, 1)

                    slice_b(l * NB, 0, 0)
                    eng.wait_ge(d1_in, l * 16 + 16)
                    spread_dst(l * NB, 0, True)
                    with eng.Fori(0, NP - 1, 1) as i:
                        for s in range(2):
                            k = l * NB + i * 2 + s
                            slice_b(k + 1, (i * 2 + (s + 1)) * TB, 1 - s)
                            spread_dst(k + 1, 1 - s, False)
                            recur(k, i, s)
                    slice_b(l * NB + (NB - 1), (NB - 1) * TB, 1)
                    spread_dst(l * NB + (NB - 1), 1, False)
                    recur(l * NB + (NB - 2), NP - 1, 0)
                    recur(l * NB + (NB - 1), NP - 1, 1)

                    for h in range(H):
                        eng.tensor_copy(m_spread[:, h * P:(h + 1) * P],
                                        wide(mx3[1][:, TB, h:h + 1], [P, P])
                                        ).then_inc(m_wide, 1)
                    hpp = [P, H, P]
                    jw3 = jw[:, :].rearrange("p (h q) -> p h q", h=H)
                    eng.wait_ge(m_turned, l + 1)
                    eng.tensor_tensor(jw3, f_ps[0][:, :].rearrange("p (h q) -> p h q", h=H),
                                      wide(apart[:, :].rearrange("p (o q) -> p o q", o=1), hpp),
                                      ALU.add).then_inc(j, 1)
                    eng.wait_ge(j, l * JS + 1)
                    eng.tensor_reduce(m_in[:, :], jw3, AX.X, ALU.max).then_inc(j, 1)
                    eng.wait_ge(j, l * JS + 2)
                    eng.tensor_tensor(jw3, jw3,
                                      wide(m_in[:, :].rearrange("p (h o) -> p h o", o=1), hpp),
                                      ALU.subtract).then_inc(j, 1)
                    eng.wait_ge(j_exp1, l + 1)
                    eng.tensor_tensor(jw3, jw3,
                                      wide(joined[:, :].rearrange("p (o q) -> p o q", o=1), hpp),
                                      ALU.mult).then_inc(j, 1)
                    eng.wait_ge(jw_turned, l + 1)
                    eng.tensor_copy(jwT[:, :], f_ps[1][:, :]).then_inc(j, 1)
                    eng.wait_ge(end_in, l * 32 + 32)
                    eng.tensor_tensor(m_all[:, :], m_in[:, :], m_end[:, :], ALU.max
                                      ).then_inc(j, 1)
                    eng.wait_ge(j, l * JS + 6)
                    eng.tensor_tensor(j_exp[:, 0, :], m_in[:, :], m_all[:, :], ALU.subtract
                                      ).then_inc(j, 1)
                    eng.tensor_tensor(j_exp[:, 1, :], m_end[:, :], m_all[:, :], ALU.subtract
                                      ).then_inc(j, 1)
                    eng.wait_ge(j_exp2, l + 1)
                    eng.wait_ge(u_in_ready, l + 1)
                    phc = [P, H, C]
                    w_j = [wide(j_wts[:, a, :].rearrange("p (h o) -> p h o", o=1), phc)
                           for a in range(2)]
                    u_in3 = u_in[:, :].rearrange("p (h c) -> p h c", h=H)
                    u_end3 = u_end[:, :].rearrange("p (h c) -> p h c", h=H)
                    eng.tensor_tensor(u_in3, o_ps[0][:, 0:HC].rearrange("p (h c) -> p h c", h=H),
                                      w_j[0], ALU.mult).then_inc(j, 1)
                    eng.tensor_tensor(u_end3, u_end3, w_j[1], ALU.mult).then_inc(j, 1)
                    eng.wait_ge(j, l * JS + 10)
                    eng.tensor_tensor(u_end[:, :], u_end[:, :], u_in[:, :], ALU.add
                                      ).then_inc(j, 1)

                    eng.wait_ge(z_in, l * (16 * NCOL) + 16 * NCOL)
                    rden3 = rden[:, :].rearrange("q (b h) -> q b h", h=H)
                    eng.reciprocal(rden3, z4[:, :, :, D]).then_inc(nd, 1)
                    eng.wait_ge(nd, l * NS + 1)
                    eng.tensor_tensor(rden3, rden3,
                                      wide(has_edge[:, :].rearrange("q (b o) -> q b o", o=1),
                                           [NQ, NCOL, H]), ALU.mult).then_inc(nd, 1)
                    eng.wait_ge(nd, l * NS + 2)
                    eng.tensor_tensor(s4, z4[:, :, :, 0:D],
                                      wide(rden[:, :].rearrange("q (b h o) -> q b h o", h=H, o=1),
                                           [NQ, NCOL, H, D]), ALU.mult).then_inc(nd, 1)
                    eng.wait_ge(n_ready, l * len(groups) + len(groups))
                    bank = 2 * GT * P // 2 // D
                    for a, z in ((0, bank), (bank, NCOL)):
                        cp = eng.tensor_copy(nf3[:, a:z, 0:D],
                                             n_ps[0:NQ, a * D:z * D]
                                             .rearrange("q (b d) -> q b d", d=D))
                        if a == 0:
                            cp.then_inc(nd, 1)
                    cp.then_inc(nf_ready, 1)
                eng.wait_ge(nf_ready, L + 1)
                eng.tensor_tensor(x3, x3, nf3[:, :, 0:D], ALU.add).then_inc(nf_ready, 1)


_INS = ['x', 'src', 'dst', 'edge_attr_32', 'L0_gnn_W_ni', 'L0_gnn_W_nj', 'L0_gnn_W_fij',
        'L0_gnn_W_node', 'L0_gnn_attn', 'L0_gnn_bias']


def kernel(**inputs):
    import numpy as _np
    import concourse.bacc as _bacc
    from concourse import mybir as _mybir
    from concourse.bass_utils import run_bass_kernel_spmd as _run

    nc = _bacc.Bacc("TRN2", target_bir_lowering=False, num_devices=1)
    arrays, args = {}, []
    for name in _INS:
        a = _np.ascontiguousarray(inputs[name])
        arrays[f"in_{name}_dram"] = a
        args.append(nc.dram_tensor(f"in_{name}_dram", a.shape, _mybir.dt.from_np(a.dtype),
                                   kind="ExternalInput").ap())
    args.append(nc.dram_tensor("out_0_dram", inputs['x'].shape, _mybir.dt.float32,
                               kind="ExternalOutput").ap())
    egat_kernel(nc, *args)
    r = _run(nc, [arrays], core_ids=[0])
    return r.results[0]["out_0_dram"]
```

```python
from contextlib import ExitStack

import concourse.bass as bass
from concourse import mybir

F32 = mybir.dt.float32
I32 = mybir.dt.int32
ALU = mybir.AluOpType
ACT = mybir.ActivationFunctionType
AX = mybir.AxisListType

P = 128
TB = 68
GT = 4
BIG = 1e38
FAR = float(1 << 20)


def egat_kernel(nc, x, src, dst, edge_attr, W_ni, W_nj, W_fij, W_node, attn, bias, out):
    N, D = x.shape
    E = src.shape[0]
    L, H, _ = attn.shape
    HD = H * D
    C = D + 1
    HC = H * C
    K = C + 2 * D
    DST0, EF0 = C, C + D
    NB = -(-E // (P * TB))
    NB += NB % 2
    T = NB * TB
    NP = NB // 2
    NG = TB // GT
    FULL = E // T
    REST = E - FULL * T
    NQ = 125
    NCOL = N // NQ
    M = H + D
    assert NQ * NCOL == N and TB % GT == 0 and HD == P and FULL < P and E < P * T
    SLOPE = 0.2
    PAD = P * T - E
    PADR = 98
    assert PAD * D % PADR == 0 and PAD * D // PADR <= TB * HC

    nf_tab = nc.dram_tensor("nf_tab", (N, C), F32, kind="Internal").ap()
    ef_tab = nc.dram_tensor("ef_tab", (P * T, D), F32, kind="Internal").ap()
    edge_first = nc.dram_tensor("edge_first", (P * T, D), F32, kind="Internal").ap()
    u_tab = nc.dram_tensor("u_tab", (P * T, HC), F32, kind="Internal").ap()
    m_tab = nc.dram_tensor("m_tab", (P * T, H), F32, kind="Internal").ap()
    dst_tab = nc.dram_tensor("dst_tab", (P, T), F32, kind="Internal").ap()
    run_tab = nc.dram_tensor("run_tab", (N + 1, 1), F32, kind="Internal").ap()

    ef_blk = ef_tab.rearrange("(p t) d -> p (t d)", t=T)
    first_blk = edge_first.rearrange("(p t) d -> p (t d)", t=T)
    u_blk = u_tab.rearrange("(p t) c -> p (t c)", t=T)
    m_blk = m_tab.rearrange("(p t) h -> p (t h)", t=T)

    with ExitStack() as ctx:
        def sb(name, shape, dt=F32):
            return ctx.enter_context(nc.sbuf_tensor(name, shape, dt))

        def ps(name, shape):
            return ctx.enter_context(nc.psum_tensor(name, shape, F32))

        def sem(name):
            return ctx.enter_context(nc.semaphore(name))

        rows = [sb(f"rows{s}", [P, TB * K]) for s in range(2)]
        rows3 = [r[:, :].rearrange("p (t k) -> p t k", k=K) for r in rows]
        first_st = sb("first_st", [P, TB * D])
        ef_st = sb("ef_st", [P, TB * D])
        ef_new = [sb(f"ef_new{s}", [P, TB * D]) for s in range(2)]
        U = [sb(f"U{s}", [P, TB * HC]) for s in range(2)]
        U3 = [u[:, :].rearrange("p (t c) -> p t c", c=HC) for u in U]
        sc = [sb(f"sc{s}", [P, TB * H]) for s in range(2)]
        mx = [sb(f"mx{s}", [P, (TB + 1) * H]) for s in range(2)]
        expo = sb("expo", [P, 2, TB * H])
        wts = sb("wts", [P, 2, TB * H])
        same_b = [sb(f"same_b{s}", [P, TB]) for s in range(2)]
        cut_b = [sb(f"cut_b{s}", [P, TB]) for s in range(2)]
        idx = [sb(f"idx{s}", [P, TB], I32) for s in range(2)]
        xT = [sb(f"xT{s}", [P, GT * P]) for s in range(2)]
        f_low = [sb(f"f_low{s}", [P, GT * P]) for s in range(2)]
        lr = [sb(f"lr{s}", [P, GT * P]) for s in range(2)]
        src_sb = sb("src_sb", [P, T], I32)
        same = sb("same", [P, T])
        cut = sb("cut", [P, T])
        ident = sb("ident", [P, P])
        nf = sb("nf", [NQ, NCOL * C])
        nf3 = nf[:, :].rearrange("q (b c) -> q b c", c=C)
        x_sb = sb("x_sb", [NQ, NCOL * D])
        w_edge = sb("w_edge", [K, HD])
        w_out = sb("w_out", [P, M])
        w_node = sb("w_node", [P, D])
        w_mean = sb("w_mean", [P, D])
        first_idx = sb("first_idx", [NQ, NCOL], I32)
        last_idx = sb("last_idx", [NQ, NCOL], I32)
        has_edge = sb("has_edge", [NQ, NCOL])
        d1_idx = sb("d1_idx", [P, 1], I32)
        joined = sb("joined", [P, P])
        apart = sb("apart", [P, P])
        end_get = sb("end_get", [P, 1], I32)
        end_put = sb("end_put", [P, 1], I32)
        nf_d1 = sb("nf_d1", [P, C])
        m_spread = sb("m_spread", [P, H * P])
        jw = sb("jw", [P, H * P])
        jwT = sb("jwT", [P, H * P])
        m_in = sb("m_in", [P, H])
        m_end = sb("m_end", [P, H])
        m_all = sb("m_all", [P, H])
        j_exp = sb("j_exp", [P, 2, H])
        j_wts = sb("j_wts", [P, 2, H])
        u_end = sb("u_end", [P, HC])
        u_in = sb("u_in", [P, HC])
        rden = sb("rden", [NQ, NCOL * H])

        xT_ps = [ps(f"xT_ps{s}", [P, GT * P]) for s in range(2)]
        f_ps = [ps(f"f_ps{s}", [P, GT * P]) for s in range(2)]
        o_ps = [ps(f"o_ps{s}", [P, GT * P]) for s in range(2)]
        n_ps = ps("n_ps", [P, 2 * GT * P])

        z4 = U[0][0:NQ, 0:NCOL * HC].rearrange("q (b h c) -> q b h c", h=H, c=C)
        s4 = U[1][0:NQ, 0:NCOL * HD].rearrange("q (b h d) -> q b h d", h=H, d=D)

        dcol = U[0][:, 0:T + 1].bitcast(I32)
        dcolf = U[1][:, 0:T + 1]
        xmp = jw[:, 0:P].bitcast(I32)
        first_f, next_f, node_f, part_f = (rden[:, a * NCOL:(a + 1) * NCOL] for a in range(4))
        mean = m_spread[0:NQ, 0:NCOL]
        var = m_spread[0:NQ, NCOL:2 * NCOL]
        xc = ef_new[0][0:NQ, 0:NCOL * D].rearrange("q (b d) -> q b d", d=D)
        xsq = ef_new[1][0:NQ, 0:NCOL * D].rearrange("q (b d) -> q b d", d=D)
        x3 = x_sb[:, :].rearrange("q (b d) -> q b d", d=D)
        first3 = first_st[:, :].rearrange("p (t d) -> p t d", d=D)
        sc3 = [a[:, :].rearrange("p (t h) -> p t h", h=H) for a in sc]
        mx3 = [a[:, :].rearrange("p (t h) -> p t h", h=H) for a in mx]

        zeroed = sem("zeroed")
        made = sem("made")
        dst_in = sem("dst_in")
        src_in = sem("src_in")
        x_in = sem("x_in")
        prep = sem("prep")
        lasts_t = sem("lasts_t")
        rooted = sem("rooted")
        dst_out = sem("dst_out")
        chunk_idx = sem("chunk_idx")
        chunk_in = [sem(f"chunk_in{s}") for s in range(2)]
        counted = sem("counted")
        run_out = sem("run_out")
        run_in = sem("run_in")
        run_end_in = sem("run_end_in")
        first_zero = sem("first_zero")
        nf_ready = sem("nf_ready")
        tab_out = sem("tab_out")
        w_in = sem("w_in")
        w_used = sem("w_used")
        first_out = sem("first_out")
        d1_in = sem("d1_in")
        idx_copied = sem("idx_copied")
        src_rows = [[sem(f"src_rows{s}_{a}") for a in range(4)] for s in range(2)]
        ef_in = sem("ef_in")
        first_in = sem("first_in")
        ef_spread = sem("ef_spread")
        dst_spread = sem("dst_spread")
        turned = sem("turned")
        xT_ready = sem("xT_ready")
        f_ready = sem("f_ready")
        f_low_ready = sem("f_low_ready")
        lr_ready = sem("lr_ready")
        o_ready = sem("o_ready")
        sc_ready = sem("sc_ready")
        ef_out = [sem(f"ef_out{s}") for s in range(2)]
        max_done = sem("max_done")
        expo_done = sem("expo_done")
        wts_ready = sem("wts_ready")
        prod_done = sem("prod_done")
        sums_done = sem("sums_done")
        u_out = [sem(f"u_out{s}") for s in range(2)]
        sliced = sem("sliced")
        normed = sem("normed")
        m_wide = sem("m_wide")
        m_turned = sem("m_turned")
        end_in = sem("end_in")
        j = sem("j")
        j_exp1 = sem("j_exp1")
        jw_turned = sem("jw_turned")
        u_in_ready = sem("u_in_ready")
        j_exp2 = sem("j_exp2")
        u_fixed = sem("u_fixed")
        z_in = sem("z_in")
        nd = sem("nd")
        s_turned = sem("s_turned")
        sT_ready = sem("sT_ready")
        n_ready = sem("n_ready")
        x_out = sem("x_out")

        passed = {e: sem(f"passed_{e}") for e in ("sp", "pool", "pe")}

        EFI = (16, 32)
        UI = (32, 16)
        DB = NQ
        AHEAD = 2
        HEAD = (NG + 1) // 2
        LEAKY_EVERY = 16

        def steps(i, span, last, turn, edges, scores):
            for jj in span:
                for stage, q in ((turn, jj + AHEAD), (edges, jj + AHEAD - 1), (scores, jj)):
                    for m in (2 * q, 2 * q + 1):
                        if m >= 0 and not (last and m >= 2 * NG):
                            stage(i + m // (2 * NG), m // NG % 2, m % NG)

        part_groups = [NG // 4 + (a >= 4 - NG % 4) for a in range(4)]
        part_of = [a for a in range(4) for _ in range(part_groups[a])]
        groups = [range(g, min(g + GT, NCOL)) for g in range(0, NCOL, GT)]
        JS, NS = 11, 4
        WI = 16 * (4 + 2 * H)

        with nc.Block() as block:

            @block.sync
            def _(eng):
                eng.wait_ge(zeroed, 3)
                eng.dma_start(dcol[0:FULL, 1:T + 1],
                              dst[0:FULL * T].rearrange("(p t) -> p t", t=T)).then_inc(dst_in, 16)
                eng.dma_start(dcol[FULL:FULL + 1, 1:REST + 1],
                              dst[FULL * T:E].rearrange("(p t) -> p t", p=1)).then_inc(dst_in, 16)
                eng.dma_start(dcol[1:FULL + 1, 0:1],
                              dst[T - 1:FULL * T].rearrange("(p t) -> p t", t=1)[::T, :]
                              , allow_slow_non_contiguous=True).then_inc(dst_in, 16)
                eng.dma_start(src_sb[0:FULL, :],
                              src[0:FULL * T].rearrange("(p t) -> p t", t=T)).then_inc(src_in, 16)
                eng.dma_start(src_sb[FULL:FULL + 1, 0:REST],
                              src[FULL * T:E].rearrange("(p t) -> p t", p=1)).then_inc(src_in, 16)
                eng.dma_start(x_sb[:, :],
                              x.rearrange("(q b) d -> q (b d)", b=NCOL)).then_inc(x_in, 16)
                eng.wait_ge(prep, 1)
                eng.dma_start(dst_tab[:, :], U[1][:, 1:T + 1]).then_inc(dst_out, 16)
                eng.dma_start(ef_tab[0:FULL * T, :].rearrange("(p t) d -> p (t d)", t=T),
                              edge_attr[0:FULL * T, :].rearrange("(p t) d -> p (t d)", t=T)
                              ).then_inc(ef_out[0], 16)
                eng.dma_start(ef_tab[FULL * T:E, :], edge_attr[FULL * T:E, :]
                              ).then_inc(ef_out[1], 16)
                eng.wait_ge(prep, 12)
                eng.dma_start(run_tab[0:N, :].rearrange("(q b) o -> q (b o)", b=NCOL),
                              rden[:, 0:NCOL]).then_inc(run_out, 16)
                eng.dma_start(run_tab[N:N + 1, :], u_end[0:1, 0:1]).then_inc(run_out, 16)
                eng.wait_ge(run_out, 32)
                eng.dma_start(rden[:, NCOL:2 * NCOL],
                              run_tab[1:N + 1, :].rearrange("(q b) o -> q (b o)", b=NCOL)
                              ).then_inc(run_in, 16)
                eng.wait_ge(zeroed, 6)
                w = TB * HC
                eng.dma_start(first_blk[:, 0:w], U[0][:, :]).then_inc(u_out[0], 16)
                eng.dma_start(first_blk[:, w:2 * w], U[0][:, :]).then_inc(u_out[0], 16)
                eng.dma_start(first_blk[:, 2 * w:T * D], U[1][:, 0:T * D - 2 * w]
                              ).then_inc(u_out[1], 16)
                eng.dma_start(ef_tab[E:P * T, :].rearrange("a d -> (a d)")
                              .rearrange("(r w) -> r w", r=PADR),
                              U[1][0:PADR, 0:PAD * D // PADR]).then_inc(ef_out[1], 16)
                eng.wait_ge(u_out[0], UI[0])
                eng.wait_ge(u_out[1], UI[1])
                eng.wait_ge(ef_out[1], EFI[1])
                eng.sem_inc(first_zero, 1)

                with eng.Fori(0, L, 1) as l:
                    eng.wait_ge(w_used, l + 1)
                    eng.wait_ge(o_ready, l * (NB * NG) + 2)
                    eng.sem_inc(passed["sp"], 1)
                    lw = bass.ds(l, 1)

                    def one(ap):
                        return ap.rearrange("a b c -> (a b) c")
                    eng.dma_start(w_edge[0:D, :], one(W_ni[lw, :, :])).then_inc(w_in, 16)
                    eng.dma_start(w_edge[D:C, :], bias[lw, :]).then_inc(w_in, 16)
                    eng.dma_start(w_edge[DST0:EF0, :], one(W_nj[lw, :, :])).then_inc(w_in, 16)
                    eng.dma_start(w_edge[EF0:K, :], one(W_fij[lw, :, :])).then_inc(w_in, 16)
                    for h in range(H):
                        eng.dma_start(w_out[h * D:(h + 1) * D, h:h + 1],
                                      attn[lw, h, :].rearrange("a d -> d a"),
                                      allow_slow_non_contiguous=True).then_inc(w_in, 16)
                        eng.dma_start(w_node[h * D:(h + 1) * D, :],
                                      one(W_node[lw, :, h * D:(h + 1) * D])).then_inc(w_in, 16)
                    eng.wait_ge(nf_ready, l + 1)
                    eng.dma_start(nf_tab.rearrange("(q b) c -> q (b c)", b=NCOL), nf[:, :]
                                  ).then_inc(tab_out, 16)
                    eng.wait_ge(ef_out[0], l * (16 * NP) + EFI[0])
                    eng.sem_inc(passed["sp"], 1)
                    eng.wait_ge(ef_out[1], l * (16 * NP) + EFI[1])
                    eng.wait_ge(first_out, l * (16 * NCOL) + 16 * NCOL)
                    eng.sem_inc(passed["sp"], 1)

                    def load(k, col):
                        eng.wait_ge(ef_spread, k)
                        eng.dma_start(ef_st[:, :], ef_blk[:, bass.ds(col, TB * D)]
                                      ).then_inc(ef_in, 16)
                        eng.wait_ge(dst_spread, k * D)
                        eng.dma_start(first_st[:, :], first_blk[:, bass.ds(col, TB * D)]
                                      ).then_inc(first_in, 16)

                    def store(k, b):
                        s = k[1]
                        eng.wait_ge(sums_done, k[0] * HC + (l + (HC + 1)))
                        eng.dma_start(u_blk[:, bass.ds(b * (TB * HC), TB * HC)], U[s][:, :]
                                      ).then_inc(u_out[s], 16)
                        eng.dma_start(m_blk[:, bass.ds(b * (TB * H), TB * H)], mx[s][:, H:]
                                      ).then_inc(u_out[s], 16)

                    load(l * NB + 1, 0)
                    load(l * NB + 2, TB * D)
                    with eng.Fori(0, NP - 1, 1) as i:
                        for s in range(2):
                            k = l * NB + i * 2 + s
                            load(k + 3, (i * 2 + (s + 2)) * (TB * D))
                            store((k, s), i * 2 + s)
                    for s in range(2):
                        store((l * NB + (NB - 2 + s), s), NB - 2 + s)
                eng.wait_ge(nf_ready, L + 2)
                eng.dma_start(out.rearrange("(q b) d -> q (b d)", b=NCOL), x_sb[:, :]
                              ).then_inc(x_out, 16)
                eng.wait_ge(x_out, 16)
                eng.wait_ge(ef_out[0], EFI[0] + 16 * NP * L)
                eng.wait_ge(ef_out[1], EFI[1] + 16 * NP * L)

            @block.gpsimd
            def _(eng):
                eng.iota(jw[:, 0:P].bitcast(I32), pattern=[[1, P]], base=0, channel_multiplier=-1
                         ).then_inc(made, 1)
                eng.iota(first_idx[:, :], pattern=[[1, NCOL]], base=0, channel_multiplier=NCOL
                         ).then_inc(made, 1)
                eng.iota(end_get[:, :], pattern=[[0, 1]], base=0, channel_multiplier=T
                         ).then_inc(made, 1)
                eng.wait_ge(dst_out, 16)
                eng.wait_ge(chunk_idx, 1)
                for b in range(NCOL):
                    if b >= 2:
                        eng.wait_ge(counted, b - 1)
                    eng.indirect_dma_start(rows[b % 2][0:NQ, 0:T], None, dst_tab[:, :],
                                           bass.IndirectOffsetOnAxis(
                                               ap=last_idx[:, b:b + 1], axis=0)
                                           ).then_inc(chunk_in[b % 2], 16)
                eng.wait_ge(run_out, 32)
                eng.wait_ge(prep, 13)
                eng.indirect_dma_start(m_in[:, 0:1], None, run_tab[:, :],
                                       bass.IndirectOffsetOnAxis(ap=d1_idx[:, 0:1], axis=0)
                                       ).then_inc(run_end_in, 16)
                eng.wait_ge(prep, 30)
                eng.wait_ge(src_in, 32)
                eng.wait_ge(first_zero, 1)

                with eng.Fori(0, L, 1) as l:
                    eng.wait_ge(nf_ready, l + 1)
                    eng.sem_inc(passed["pool"], 1)
                    for b in range(NCOL):
                        eng.indirect_dma_start(edge_first[:, :],
                                               bass.IndirectOffsetOnAxis(
                                                   ap=first_idx[:, b:b + 1], axis=0),
                                               nf[:, b * C:b * C + D], None,
                                               bounds_check=P * T - 1, oob_is_err=False
                                               ).then_inc(first_out, 16)
                    eng.wait_ge(tab_out, l * 16 + 16)
                    eng.sem_inc(passed["pool"], 1)
                    eng.indirect_dma_start(nf_d1[:, :], None, nf_tab[:, :],
                                           bass.IndirectOffsetOnAxis(ap=d1_idx[:, 0:1], axis=0)
                                           ).then_inc(d1_in, 16)
                    with eng.Fori(0, NP, 1) as i:
                        for s in range(2):
                            k = l * NB + i * 2 + s
                            eng.wait_ge(turned, k * NG + NG)
                            eng.wait_ge(prod_done, k * 2 + 2)
                            eng.tensor_copy(idx[s][:, :],
                                            src_sb[:, bass.ds((i * 2 + s) * TB, TB)]
                                            ).then_inc(idx_copied, 1)
                            eng.wait_ge(idx_copied, k + 1)
                            eng.sem_inc(passed["pool"], 1)
                            for t in range(TB):
                                eng.indirect_dma_start(rows[s][:, t * K:t * K + C], None,
                                                       nf_tab[:, :],
                                                       bass.IndirectOffsetOnAxis(
                                                           ap=idx[s][:, t:t + 1], axis=0)
                                                       ).then_inc(
                                                           src_rows[s][part_of[t // GT]], 16)
                    eng.wait_ge(u_out[0], l * (32 * NP) + (UI[0] + 32 * NP))
                    eng.wait_ge(u_out[1], l * (32 * NP) + (UI[1] + 32 * NP))
                    eng.sem_inc(passed["pool"], 1)
                    eng.indirect_dma_start(u_end[:, :], None, u_tab[:, :],
                                           bass.IndirectOffsetOnAxis(ap=end_get[:, 0:1], axis=0)
                                           ).then_inc(end_in, 16)
                    eng.indirect_dma_start(m_end[:, :], None, m_tab[:, :],
                                           bass.IndirectOffsetOnAxis(ap=end_get[:, 0:1], axis=0)
                                           ).then_inc(end_in, 16)
                    eng.wait_ge(j, l * JS + JS)
                    eng.sem_inc(passed["pool"], 1)
                    eng.indirect_dma_start(u_tab[:, :],
                                           bass.IndirectOffsetOnAxis(ap=end_put[:, 0:1], axis=0),
                                           u_end[:, :], None,
                                           bounds_check=P * T - 1, oob_is_err=False
                                           ).then_inc(u_fixed, 16)
                    eng.wait_ge(u_fixed, l * 16 + 16)
                    eng.sem_inc(passed["pool"], 1)
                    for b in range(NCOL):
                        eng.indirect_dma_start(U[0][0:NQ, b * HC:(b + 1) * HC], None,
                                               u_tab[:, :],
                                               bass.IndirectOffsetOnAxis(
                                                   ap=last_idx[:, b:b + 1], axis=0)
                                               ).then_inc(z_in, 16)

            @block.tensor
            def _(eng):
                eng.wait_ge(prep, 3)
                eng.transpose(f_ps[0][:, 0:P], jwT[:, 0:P], ident[:, :]).then_inc(lasts_t, 1)
                eng.sem_inc(turned, 2 * NG)
                eng.sem_inc(f_ready, 2)
                eng.sem_inc(o_ready, 2)

                with eng.Fori(0, L, 1) as l:
                    eng.wait_ge(w_in, l * WI + WI)
                    eng.sem_inc(passed["pe"], 1)

                    def turn(i, s, g):
                        n, y = (l * NB + i * 2 + s) * NG + g, (s * NG + g) % 2
                        if g == 0:
                            k = l * NB + i * 2 + s
                            eng.wait_ge(dst_spread, k * D + 2 * D)
                            eng.wait_ge(ef_spread, k + 2)
                        a = part_of[g]
                        w = 16 * GT * part_groups[a]
                        if g == 0 or part_of[g - 1] != a:
                            eng.wait_ge(src_rows[s][a], (l * NP + i) * w + w)
                        eng.wait_ge(xT_ready, n + 1)
                        for u in range(GT):
                            mm = eng.transpose(xT_ps[y][0:K, u * P:(u + 1) * P],
                                               rows3[s][:, g * GT + u, :], ident[:, :])
                        mm.then_inc(turned, 1)

                    def edges(i, s, g):
                        n, y = (l * NB + i * 2 + s) * NG + g, (s * NG + g) % 2
                        eng.wait_ge(xT_ready, n + 3)
                        eng.wait_ge(lr_ready, n + 1)
                        eng.matmul(f_ps[y][:, :], w_edge[:, :], xT[y][0:K, :],
                                   start=True, stop=True).then_inc(f_ready, 1)

                    def scores(i, s, g):
                        n, y = (l * NB + i * 2 + s) * NG + g, (s * NG + g) % 2
                        eng.wait_ge(lr_ready, n + 3)
                        eng.wait_ge(sc_ready, n * 2 + 2)
                        for u in range(GT):
                            mm = eng.matmul(o_ps[y][:, u * M:(u + 1) * M],
                                            lr[y][:, u * P:(u + 1) * P], w_out[:, :],
                                            start=True, stop=True)
                        mm.then_inc(o_ready, 1)

                    steps(0, range(-AHEAD, 0), False, turn, edges, scores)
                    with eng.Fori(0, NP - 1, 1) as i:
                        steps(i, range(NG), False, turn, edges, scores)
                    steps(NP - 1, range(NG), True, turn, edges, scores)
                    eng.wait_ge(m_wide, l * H + H)
                    for h in range(H):
                        mm = eng.transpose(f_ps[0][:, h * P:(h + 1) * P],
                                           m_spread[:, h * P:(h + 1) * P], ident[:, :])
                    mm.then_inc(m_turned, 1)
                    eng.wait_ge(j, l * JS + 4)
                    for h in range(H):
                        mm = eng.transpose(f_ps[1][:, h * P:(h + 1) * P],
                                           jw[:, h * P:(h + 1) * P], ident[:, :])
                    mm.then_inc(jw_turned, 1)
                    eng.wait_ge(j, l * JS + 5)
                    for h in range(H):
                        mm = eng.matmul(o_ps[0][:, h * C:(h + 1) * C],
                                        jwT[:, h * P:(h + 1) * P],
                                        U3[1][:, TB - 1, h * C:(h + 1) * C],
                                        start=True, stop=True)
                    mm.then_inc(u_in_ready, 1)
                    eng.wait_ge(nd, l * NS + 3)

                    def node_turn(n):
                        if n >= 2:
                            eng.wait_ge(sT_ready, l * len(groups) + (n - 1))
                        for u, b in enumerate(groups[n]):
                            mm = eng.transpose(xT_ps[n % 2][:, u * DB:(u + 1) * DB],
                                               U[1][0:NQ, b * HD:(b + 1) * HD],
                                               ident[0:NQ, 0:NQ])
                        mm.then_inc(s_turned, 1)

                    node_turn(0)
                    for n in range(len(groups)):
                        if n + 1 < len(groups):
                            node_turn(n + 1)
                        eng.wait_ge(sT_ready, l * len(groups) + (n + 1))
                        for u, b in enumerate(groups[n]):
                            mm = eng.matmul(n_ps[0:NQ, b * D:(b + 1) * D],
                                            xT[n % 2][:, u * DB:(u + 1) * DB], w_mean[:, :],
                                            start=True, stop=True)
                        mm.then_inc(n_ready, 1)

            @block.scalar
            def _(eng):
                eng.sem_inc(xT_ready, 2)
                eng.sem_inc(sc_ready, 4)
                eng.sem_inc(ef_spread, 1)
                eng.wait_ge(normed, 5)
                eng.activation(var, var, ACT.Sqrt).then_inc(rooted, 1)

                with eng.Fori(0, L, 1) as l:
                    def spread(k, s):
                        eng.wait_ge(ef_in, k * 16 + 16)
                        eng.wait_ge(turned, k * NG + NG)
                        eng.activation(rows3[s][:, :, EF0:K],
                                       ef_st[:, :].rearrange("p (t d) -> p t d", d=D),
                                       ACT.Copy).then_inc(ef_spread, 1)

                    def take_xT(i, s, g):
                        n, y = (l * NB + i * 2 + s) * NG + g, (s * NG + g) % 2
                        eng.wait_ge(turned, n + 2 * NG + 1)
                        eng.wait_ge(f_ready, n + 1)
                        eng.activation(xT[y][0:K, :], xT_ps[y][0:K, :], ACT.Copy
                                       ).then_inc(xT_ready, 1)

                    def lower(i, s, g):
                        n, y = (l * NB + i * 2 + s) * NG + g, (s * NG + g) % 2
                        eng.wait_ge(f_ready, n + 3)
                        eng.wait_ge(lr_ready, n + 1)
                        eng.activation(f_low[y][:, :], f_ps[y][:, :], ACT.Copy, scale=SLOPE
                                       ).then_inc(f_low_ready, 1)

                    def weigh(k):
                        eng.wait_ge(expo_done, k * 3 + 3)
                        eng.activation(wts[:, :, :], expo[:, :, :], ACT.Exp).then_inc(wts_ready, 1)

                    def take_scores(i, s, g, first, last):
                        k = l * NB + i * 2 + s
                        n, y = k * NG + g, (s * NG + g) % 2
                        if g == 0:
                            eng.wait_ge(prod_done, k * 2 + 2)
                            eng.wait_ge(ef_out[s], (l * NP + i) * 16 + EFI[s])
                        eng.wait_ge(o_ready, n + 3)
                        o3 = o_ps[y][:, 0:GT * M].rearrange("p (t m) -> p t m", m=M)
                        eng.activation(sc[s][:, g * GT * H:(g + 1) * GT * H]
                                       .rearrange("p (t h) -> p t h", h=H),
                                       o3[:, :, 0:H], ACT.Copy).then_inc(sc_ready, 1)
                        eng.activation(ef_new[s][:, g * GT * D:(g + 1) * GT * D]
                                       .rearrange("p (t d) -> p t d", d=D),
                                       o3[:, :, H:M], ACT.Copy).then_inc(sc_ready, 1)
                        if g == 0 and not first:
                            weigh(k - 1)
                        if g == NG // 3 and not (last and s == 1):
                            spread(k + 1, 1 - s)
                        if g == NG - 1:
                            eng.wait_ge(sc_ready, k * (2 * NG) + (2 * NG + 4))
                            eng.dma_start(ef_blk[:, bass.ds((i * 2 + s) * (TB * D), TB * D)],
                                          ef_new[s][:, :]).then_inc(ef_out[s], 16)

                    spread(l * NB, 0)
                    steps(0, range(-AHEAD, HEAD), False, take_xT, lower,
                          lambda i, s, g: take_scores(i, s, g, s == 0, False))
                    with eng.Fori(0, NP - 1, 1) as i:
                        steps(i, range(HEAD, NG + HEAD), False, take_xT, lower,
                              lambda i, s, g: take_scores(i, s, g, False, False))
                    steps(NP - 1, range(HEAD, NG), True, take_xT, lower,
                          lambda i, s, g: take_scores(i, s, g, False, True))
                    weigh(l * NB + (NB - 1))

                    eng.wait_ge(j, l * JS + 3)
                    eng.activation(jw[:, :], jw[:, :], ACT.Exp).then_inc(j_exp1, 1)
                    eng.wait_ge(j, l * JS + 8)
                    eng.activation(j_wts[:, :, :], j_exp[:, :, :], ACT.Exp).then_inc(j_exp2, 1)
                    for n in range(len(groups)):
                        w = len(groups[n]) * DB
                        eng.wait_ge(s_turned, l * len(groups) + (n + 1))
                        if n >= 2:
                            eng.wait_ge(n_ready, l * len(groups) + (n - 1))
                        eng.activation(xT[n % 2][:, 0:w], xT_ps[n % 2][:, 0:w], ACT.Copy
                                       ).then_inc(sT_ready, 1)

            @block.vector
            def _(eng):
                def wide(ap, shape):
                    return ap.broadcast_to(shape)

                eng.memset(dcol, N).then_inc(zeroed, 1)
                eng.memset(src_sb[:, :], 0).then_inc(zeroed, 1)
                eng.wait_ge(zeroed, 2)
                eng.memset(dcol[0:1, 0:1], -1).then_inc(zeroed, 1)
                eng.memset(u_end[:, :], float(E)).then_inc(zeroed, 1)
                eng.sem_inc(lr_ready, 2)
                eng.sem_inc(prod_done, 4)
                eng.sem_inc(dst_spread, D)
                eng.wait_ge(dst_in, 48)
                eng.tensor_copy(dcolf, dcol).then_inc(prep, 1)
                eng.wait_ge(made, 3)
                eng.tensor_scalar(ident[:, :], xmp, 0.0, None, ALU.is_equal).then_inc(prep, 1)
                eng.wait_ge(prep, 1)
                eng.tensor_copy(jwT[:, 0:P], wide(dcolf[:, T:T + 1], [P, P])).then_inc(prep, 1)
                eng.tensor_tensor(same[:, :], dcolf[:, 1:T + 1], dcolf[:, 0:T], ALU.is_equal
                                  ).then_inc(prep, 1)
                eng.wait_ge(prep, 4)
                eng.tensor_scalar(cut[:, :], same[:, :], -1.0, BIG, ALU.add, ALU.mult
                                  ).then_inc(prep, 1)
                eng.tensor_copy(node_f, first_idx[:, :]).then_inc(prep, 1)
                eng.wait_ge(prep, 6)
                eng.wait_ge(lasts_t, 1)
                below = U[0][0:NQ, 0:NCOL * P].rearrange("q (b p) -> q b p", p=P)
                eng.tensor_tensor(below,
                                  wide(f_ps[0][0:NQ, 0:P].rearrange("q (o p) -> q o p", o=1),
                                       [NQ, NCOL, P]),
                                  wide(node_f.rearrange("q (b o) -> q b o", o=1), [NQ, NCOL, P]),
                                  ALU.is_lt).then_inc(prep, 1)
                eng.wait_ge(prep, 7)
                eng.tensor_reduce(part_f, below, AX.X, ALU.add).then_inc(prep, 1)
                eng.wait_ge(prep, 8)
                eng.tensor_copy(last_idx[:, :], part_f).then_inc(chunk_idx, 1)
                eng.tensor_scalar(jwT[:, P:2 * P], xmp, 0.0, None, ALU.is_lt).then_inc(prep, 1)
                eng.wait_ge(prep, 9)
                eng.scalar_tensor_tensor(joined[:, :], f_ps[0][:, 0:P], dcolf[:, 1:2],
                                         jwT[:, P:2 * P], ALU.is_equal, ALU.mult
                                         ).then_inc(prep, 1)
                eng.wait_ge(prep, 10)
                eng.tensor_scalar(apart[:, :], joined[:, :], -1.0, BIG, ALU.add, ALU.mult
                                  ).then_inc(prep, 1)
                for b in range(NCOL):
                    eng.wait_ge(chunk_in[b % 2], 16 * (b // 2 + 1))
                    eng.tensor_scalar(U[0][0:NQ, (b % 2) * T:(b % 2 + 1) * T],
                                      rows[b % 2][0:NQ, 0:T], node_f[:, b:b + 1], None,
                                      ALU.is_lt, ALU.add, accum_out=first_f[:, b:b + 1]
                                      ).then_inc(counted, 1)
                eng.wait_ge(counted, NCOL)
                eng.scalar_tensor_tensor(first_f, part_f, float(T), first_f, ALU.mult, ALU.add
                                         ).then_inc(prep, 1)
                eng.tensor_scalar(d1_idx[:, :], dcolf[:, 1:2], 1.0, float(N), ALU.add, ALU.min
                                  ).then_inc(prep, 1)
                eng.wait_ge(dst_out, 16)
                eng.tensor_copy(m_in[:, 1:2], end_get[:, :]).then_inc(prep, 1)
                eng.tensor_scalar(m_in[:, 2:3], dcolf[:, 1:2], float(N - 1), None, ALU.min
                                  ).then_inc(prep, 1)
                eng.wait_ge(prep, 15)
                eng.memset(U[0][:, :], 0.0).then_inc(zeroed, 1)
                eng.memset(U[1][:, :], 0.0).then_inc(zeroed, 1)
                eng.wait_ge(x_in, 16)
                wide_q = [NQ, NCOL, D]
                eng.tensor_reduce(mean, x3, AX.X, ALU.add).then_inc(normed, 1)
                eng.wait_ge(normed, 1)
                eng.tensor_scalar(mean, mean, 1.0 / D, None, ALU.mult).then_inc(normed, 1)
                eng.wait_ge(normed, 2)
                mean_w = wide(mean.rearrange("q (b o) -> q b o", o=1), wide_q)
                var_w = wide(var.rearrange("q (b o) -> q b o", o=1), wide_q)
                eng.tensor_tensor(xc, x3, mean_w, ALU.subtract).then_inc(normed, 1)
                eng.wait_ge(normed, 3)
                eng.tensor_tensor(xsq, xc, xc, ALU.mult).then_inc(normed, 1)
                eng.wait_ge(normed, 4)
                eng.tensor_reduce(var, xsq, AX.X, ALU.add).then_inc(prep, 1)
                eng.wait_ge(prep, 16)
                eng.tensor_scalar(var, var, 1.0 / D, 1e-5, ALU.mult, ALU.add).then_inc(normed, 1)
                eng.wait_ge(rooted, 1)
                eng.reciprocal(var, var).then_inc(normed, 1)
                eng.wait_ge(normed, 6)
                eng.tensor_tensor(xc, xc, var_w, ALU.mult).then_inc(normed, 1)
                eng.wait_ge(normed, 7)
                eng.memset(nf3[:, :, D:C], 1.0)
                eng.tensor_scalar(nf3[:, :, 0:D], xc, 0.0, None, ALU.max).then_inc(nf_ready, 1)
                eng.memset(w_out[:, :], 0.0).then_inc(prep, 1)
                eng.wait_ge(prep, 17)
                eng.tensor_reduce(w_out[:, H:M], ident[:, :].rearrange("p (h d) -> p d h", d=D),
                                  AX.X, ALU.add).then_inc(prep, 1)
                eng.wait_ge(prep, 18)
                eng.tensor_scalar(w_out[:, H:M], w_out[:, H:M], 1.0 / H, None, ALU.mult
                                  ).then_inc(w_used, 1)
                eng.wait_ge(run_in, 16)
                eng.wait_ge(run_end_in, 16)
                eng.tensor_tensor(has_edge[:, :], first_f, next_f, ALU.is_lt).then_inc(prep, 1)
                eng.wait_ge(prep, 19)
                eng.scalar_tensor_tensor(last_idx[:, :], next_f, -1.0, has_edge[:, :],
                                         ALU.add, ALU.mult).then_inc(prep, 1)
                eng.tensor_scalar(part_f, has_edge[:, :], -FAR, FAR, ALU.mult, ALU.add
                                  ).then_inc(prep, 1)
                eng.wait_ge(prep, 21)
                eng.tensor_tensor(first_idx[:, :], part_f, first_f, ALU.add).then_inc(prep, 1)
                col, here = m_end[:, 0:1], m_end[:, 1:2]
                eng.scalar_tensor_tensor(col, m_in[:, 0:1], -1.0, m_in[:, 1:2],
                                         ALU.add, ALU.subtract).then_inc(prep, 1)
                eng.wait_ge(prep, 23)
                eng.tensor_scalar(here, col, 0.0, None, ALU.is_ge).then_inc(prep, 1)
                eng.wait_ge(prep, 24)
                eng.scalar_tensor_tensor(here, col, float(T), here, ALU.is_lt, ALU.mult
                                         ).then_inc(prep, 1)
                eng.wait_ge(prep, 25)
                eng.tensor_tensor(m_end[:, 2:3], col, here, ALU.mult).then_inc(prep, 1)
                eng.tensor_scalar(m_end[:, 3:4], here, -FAR, FAR, ALU.mult, ALU.add
                                  ).then_inc(prep, 1)
                eng.wait_ge(prep, 27)
                eng.tensor_tensor(end_get[:, :], m_in[:, 1:2], m_end[:, 2:3], ALU.add
                                  ).then_inc(prep, 1)
                eng.scalar_tensor_tensor(end_put[:, :], m_in[:, 0:1], -1.0, m_end[:, 3:4],
                                         ALU.add, ALU.add).then_inc(prep, 1)
                eng.tensor_copy(d1_idx[:, :], m_in[:, 2:3]).then_inc(prep, 1)
                eng.wait_ge(prep, 30)

                with eng.Fori(0, L, 1) as l:
                    eng.wait_ge(w_in, l * WI + WI)
                    eng.tensor_scalar(w_mean[:, :], w_node[:, :], 1.0 / H, None, ALU.mult
                                      ).then_inc(w_used, 1)
                    eng.memset(U3[1][:, TB - 1, :], 0.0).then_inc(sums_done, 1)
                    eng.memset(mx3[1][:, TB, :], -BIG).then_inc(max_done, 1)

                    def slice_b(k, col, s):
                        eng.tensor_copy(same_b[s][:, :], same[:, bass.ds(col, TB)]
                                        ).then_inc(sliced, 1)
                        eng.tensor_copy(cut_b[s][:, :], cut[:, bass.ds(col, TB)]
                                        ).then_inc(sliced, 1)

                    def spread_dst(k, s, first):
                        eng.wait_ge(first_in, k * 16 + 16)
                        eng.wait_ge(turned, k * NG + NG)
                        eng.wait_ge(sliced, k * 2 + 2)
                        eng.wait_ge(dst_spread, k * D + D)
                        for d in range(D):
                            before = (nf_d1[:, d:d + 1] if first
                                      else rows3[1 - s][:, TB - 1, DST0 + d:DST0 + d + 1])
                            eng.tensor_tensor_scan(rows3[s][:, :, DST0 + d], same_b[s][:, :],
                                                   first3[:, :, d], before,
                                                   ALU.mult, ALU.add).then_inc(dst_spread, 1)

                    def leaky2(n):
                        for y in range(2):
                            eng.wait_ge(f_low_ready, n + (y + 1))
                            eng.wait_ge(o_ready, n + (y + 1))
                            eng.tensor_tensor(lr[y][:, :], f_ps[y][:, :], f_low[y][:, :], ALU.max
                                              ).then_inc(lr_ready, 1)

                    def recur(k, i, s, more, spread):
                        eng.wait_ge(sc_ready, k * (2 * NG) + (2 * NG + 4))
                        eng.wait_ge(u_out[s], (l * NP + i) * 32 + UI[s])
                        eng.wait_ge(max_done, k * (H + 1) + (l + 1))
                        eng.tensor_copy(mx3[s][:, 0, :], mx3[1 - s][:, TB, :]
                                        ).then_inc(max_done, 1)
                        for h in range(H):
                            eng.tensor_tensor_scan(mx3[s][:, 1:TB + 1, h], cut_b[s][:, :],
                                                   sc3[s][:, :, h], mx3[1 - s][:, TB, h:h + 1],
                                                   ALU.add, ALU.max).then_inc(max_done, 1)
                        eng.wait_ge(max_done, k * (H + 1) + (l + (H + 2)))
                        ex = [expo[:, a, :].rearrange("p (t h) -> p t h", h=H) for a in range(2)]
                        eng.tensor_tensor(ex[0], mx3[s][:, 0:TB, :], mx3[s][:, 1:TB + 1, :],
                                          ALU.subtract).then_inc(expo_done, 1)
                        eng.tensor_tensor(ex[1], sc3[s], mx3[s][:, 1:TB + 1, :],
                                          ALU.subtract).then_inc(expo_done, 1)
                        eng.wait_ge(expo_done, k * 3 + 2)
                        eng.tensor_tensor(ex[0], ex[0],
                                          wide(cut_b[s][:, :].rearrange("p (t o) -> p t o", o=1),
                                               [P, TB, H]), ALU.add).then_inc(expo_done, 1)
                        twos = [(k + 1) * NG + g for g in range(1 - s, NG, 2)] if more else []
                        if twos:
                            leaky2(twos.pop(0))
                        eng.wait_ge(wts_ready, k + 1)
                        cut4 = [P, TB // 2, H, C]
                        for a in range(2):
                            if a and twos:
                                leaky2(twos.pop(0))
                            t = slice(a * (TB // 2), (a + 1) * (TB // 2))
                            eng.tensor_tensor(
                                U3[s][:, t, :].rearrange("p t (h c) -> p t h c", c=C),
                                wide(rows3[s][:, t, 0:C].rearrange("p t (o c) -> p t o c", o=1),
                                     cut4),
                                wide(wts[:, 1, t.start * H:t.stop * H]
                                     .rearrange("p (t h o) -> p t h o", h=H, o=1), cut4),
                                ALU.mult).then_inc(prod_done, 1)
                        eng.wait_ge(prod_done, k * 2 + 6)
                        eng.wait_ge(sums_done, k * HC + (l + 1))
                        decay = wts[:, 0, :].rearrange("p (t h) -> p t h", h=H)
                        if spread:
                            slice_b(k + 2, (i * 2 + (s + 2)) * TB, s)
                        for c in range(HC):
                            if spread and c == HC // 3:
                                spread_dst(k + 2, s, False)
                            eng.tensor_tensor_scan(U3[s][:, :, c], decay[:, :, c // C],
                                                   U3[s][:, :, c], U3[1 - s][:, TB - 1, c:c + 1],
                                                   ALU.mult, ALU.add).then_inc(sums_done, 1)
                            if twos and c % LEAKY_EVERY == 0:
                                leaky2(twos.pop(0))
                        for n in twos:
                            leaky2(n)

                    eng.wait_ge(d1_in, l * 16 + 16)
                    for s in range(2):
                        slice_b(l * NB + s, s * TB, s)
                        spread_dst(l * NB + s, s, s == 0)
                    for g in range(0, NG + 1, 2):
                        leaky2(l * NB * NG + g)
                    with eng.Fori(0, NP - 1, 1) as i:
                        for s in range(2):
                            recur(l * NB + i * 2 + s, i, s, True, True)
                    recur(l * NB + (NB - 2), NP - 1, 0, True, False)
                    recur(l * NB + (NB - 1), NP - 1, 1, False, False)

                    for h in range(H):
                        eng.tensor_copy(m_spread[:, h * P:(h + 1) * P],
                                        wide(mx3[1][:, TB, h:h + 1], [P, P])
                                        ).then_inc(m_wide, 1)
                    hpp = [P, H, P]
                    jw3 = jw[:, :].rearrange("p (h q) -> p h q", h=H)
                    eng.wait_ge(m_turned, l + 1)
                    eng.tensor_tensor(jw3, f_ps[0][:, :].rearrange("p (h q) -> p h q", h=H),
                                      wide(apart[:, :].rearrange("p (o q) -> p o q", o=1), hpp),
                                      ALU.add).then_inc(j, 1)
                    eng.wait_ge(j, l * JS + 1)
                    eng.tensor_reduce(m_in[:, :], jw3, AX.X, ALU.max).then_inc(j, 1)
                    eng.wait_ge(j, l * JS + 2)
                    eng.tensor_tensor(jw3, jw3,
                                      wide(m_in[:, :].rearrange("p (h o) -> p h o", o=1), hpp),
                                      ALU.subtract).then_inc(j, 1)
                    eng.wait_ge(j_exp1, l + 1)
                    eng.tensor_tensor(jw3, jw3,
                                      wide(joined[:, :].rearrange("p (o q) -> p o q", o=1), hpp),
                                      ALU.mult).then_inc(j, 1)
                    eng.wait_ge(jw_turned, l + 1)
                    eng.tensor_copy(jwT[:, :], f_ps[1][:, :]).then_inc(j, 1)
                    eng.wait_ge(end_in, l * 32 + 32)
                    eng.tensor_tensor(m_all[:, :], m_in[:, :], m_end[:, :], ALU.max
                                      ).then_inc(j, 1)
                    eng.wait_ge(j, l * JS + 6)
                    eng.tensor_tensor(j_exp[:, 0, :], m_in[:, :], m_all[:, :], ALU.subtract
                                      ).then_inc(j, 1)
                    eng.tensor_tensor(j_exp[:, 1, :], m_end[:, :], m_all[:, :], ALU.subtract
                                      ).then_inc(j, 1)
                    eng.wait_ge(j_exp2, l + 1)
                    eng.wait_ge(u_in_ready, l + 1)
                    phc = [P, H, C]
                    w_j = [wide(j_wts[:, a, :].rearrange("p (h o) -> p h o", o=1), phc)
                           for a in range(2)]
                    u_in3 = u_in[:, :].rearrange("p (h c) -> p h c", h=H)
                    u_end3 = u_end[:, :].rearrange("p (h c) -> p h c", h=H)
                    eng.tensor_tensor(u_in3, o_ps[0][:, 0:HC].rearrange("p (h c) -> p h c", h=H),
                                      w_j[0], ALU.mult).then_inc(j, 1)
                    eng.tensor_tensor(u_end3, u_end3, w_j[1], ALU.mult).then_inc(j, 1)
                    eng.wait_ge(j, l * JS + 10)
                    eng.tensor_tensor(u_end[:, :], u_end[:, :], u_in[:, :], ALU.add
                                      ).then_inc(j, 1)

                    eng.wait_ge(z_in, l * (16 * NCOL) + 16 * NCOL)
                    rden3 = rden[:, :].rearrange("q (b h) -> q b h", h=H)
                    eng.reciprocal(rden3, z4[:, :, :, D]).then_inc(nd, 1)
                    eng.wait_ge(nd, l * NS + 1)
                    eng.tensor_tensor(rden3, rden3,
                                      wide(has_edge[:, :].rearrange("q (b o) -> q b o", o=1),
                                           [NQ, NCOL, H]), ALU.mult).then_inc(nd, 1)
                    eng.wait_ge(nd, l * NS + 2)
                    eng.tensor_tensor(s4, z4[:, :, :, 0:D],
                                      wide(rden[:, :].rearrange("q (b h o) -> q b h o", h=H, o=1),
                                           [NQ, NCOL, H, D]), ALU.mult).then_inc(nd, 1)
                    eng.wait_ge(n_ready, l * len(groups) + len(groups))
                    bank = 2 * GT * P // 2 // D
                    for a, z in ((0, bank), (bank, NCOL)):
                        cp = eng.tensor_copy(nf3[:, a:z, 0:D],
                                             n_ps[0:NQ, a * D:z * D]
                                             .rearrange("q (b d) -> q b d", d=D))
                        if a == 0:
                            cp.then_inc(nd, 1)
                    cp.then_inc(nf_ready, 1)
                eng.wait_ge(nf_ready, L + 1)
                eng.tensor_tensor(x3, x3, nf3[:, :, 0:D], ALU.add).then_inc(nf_ready, 1)


_INS = ['x', 'src', 'dst', 'edge_attr_32', 'L0_gnn_W_ni', 'L0_gnn_W_nj', 'L0_gnn_W_fij',
        'L0_gnn_W_node', 'L0_gnn_attn', 'L0_gnn_bias']


def kernel(**inputs):
    import numpy as _np
    import concourse.bacc as _bacc
    from concourse import mybir as _mybir
    from concourse.bass_utils import run_bass_kernel_spmd as _run

    nc = _bacc.Bacc("TRN2", target_bir_lowering=False, num_devices=1)
    arrays, args = {}, []
    for name in _INS:
        a = _np.ascontiguousarray(inputs[name])
        arrays[f"in_{name}_dram"] = a
        args.append(nc.dram_tensor(f"in_{name}_dram", a.shape, _mybir.dt.from_np(a.dtype),
                                   kind="ExternalInput").ap())
    args.append(nc.dram_tensor("out_0_dram", inputs['x'].shape, _mybir.dt.float32,
                               kind="ExternalOutput").ap())
    egat_kernel(nc, *args)
    r = _run(nc, [arrays], core_ids=[0])
    return r.results[0]["out_0_dram"]
```

```python
from contextlib import ExitStack

import concourse.bass as bass
from concourse import mybir

F32 = mybir.dt.float32
I32 = mybir.dt.int32
ALU = mybir.AluOpType
ACT = mybir.ActivationFunctionType
AX = mybir.AxisListType

P = 128
TB = 68
GT = 4
BIG = 1e38
FAR = float(1 << 20)


def egat_kernel(nc, x, src, dst, edge_attr, W_ni, W_nj, W_fij, W_node, attn, bias, out):
    N, D = x.shape
    E = src.shape[0]
    L, H, _ = attn.shape
    HD = H * D
    C = D + 1
    HC = H * C
    K = C + 2 * D
    DST0, EF0 = C, C + D
    NB = -(-E // (P * TB))
    NB += NB % 2
    T = NB * TB
    NP = NB // 2
    NG = TB // GT
    FULL = E // T
    REST = E - FULL * T
    NQ = 125
    NCOL = N // NQ
    M = H + D
    assert NQ * NCOL == N and TB % GT == 0 and HD == P and FULL < P and E < P * T
    SLOPE = 0.2
    PAD = P * T - E
    PADR = 98
    assert PAD * D % PADR == 0 and PAD * D // PADR <= TB * D

    nf_tab = nc.dram_tensor("nf_tab", (N, C), F32, kind="Internal").ap()
    ef_tab = nc.dram_tensor("ef_tab", (P * T, D), F32, kind="Internal").ap()
    edge_first = nc.dram_tensor("edge_first", (P * T, D), F32, kind="Internal").ap()
    u_tab = nc.dram_tensor("u_tab", (P * T, HC), F32, kind="Internal").ap()
    m_tab = nc.dram_tensor("m_tab", (P * T, H), F32, kind="Internal").ap()
    dst_tab = nc.dram_tensor("dst_tab", (P, T), F32, kind="Internal").ap()
    run_tab = nc.dram_tensor("run_tab", (N + 1, 1), F32, kind="Internal").ap()

    ef_blk = ef_tab.rearrange("(p t) d -> p (t d)", t=T)
    first_blk = edge_first.rearrange("(p t) d -> p (t d)", t=T)
    u_blk = u_tab.rearrange("(p t) c -> p (t c)", t=T)
    m_blk = m_tab.rearrange("(p t) h -> p (t h)", t=T)

    with ExitStack() as ctx:
        def sb(name, shape, dt=F32):
            return ctx.enter_context(nc.sbuf_tensor(name, shape, dt))

        def ps(name, shape):
            return ctx.enter_context(nc.psum_tensor(name, shape, F32))

        def sem(name):
            return ctx.enter_context(nc.semaphore(name))

        rows = [sb(f"rows{s}", [P, TB * K]) for s in range(2)]
        rows3 = [r[:, :].rearrange("p (t k) -> p t k", k=K) for r in rows]
        first_st = sb("first_st", [P, TB * D])
        ef_st = sb("ef_st", [P, TB * D])
        ef_new = [sb(f"ef_new{s}", [P, TB * D]) for s in range(2)]
        U = [sb(f"U{s}", [P, TB * HC]) for s in range(2)]
        U3 = [u[:, :].rearrange("p (t c) -> p t c", c=HC) for u in U]
        sc = [sb(f"sc{s}", [P, TB * H]) for s in range(2)]
        mx = [sb(f"mx{s}", [P, (TB + 1) * H]) for s in range(2)]
        expo = sb("expo", [P, 2, TB * H])
        wts = sb("wts", [P, 2, TB * H])
        same_b = [sb(f"same_b{s}", [P, TB]) for s in range(2)]
        cut_b = [sb(f"cut_b{s}", [P, TB]) for s in range(2)]
        idx = [sb(f"idx{s}", [P, TB], I32) for s in range(2)]
        xT = [sb(f"xT{s}", [P, GT * P]) for s in range(2)]
        f_low = [sb(f"f_low{s}", [P, GT * P]) for s in range(2)]
        lr = [sb(f"lr{s}", [P, GT * P]) for s in range(2)]
        src_sb = sb("src_sb", [P, T], I32)
        same = sb("same", [P, T])
        cut = sb("cut", [P, T])
        ident = sb("ident", [P, P])
        nf = sb("nf", [NQ, NCOL * C])
        nf3 = nf[:, :].rearrange("q (b c) -> q b c", c=C)
        x_sb = sb("x_sb", [NQ, NCOL * D])
        w_edge = sb("w_edge", [K, HD])
        w_out = sb("w_out", [P, M])
        w_node = sb("w_node", [P, D])
        w_mean = sb("w_mean", [P, D])
        first_idx = sb("first_idx", [NQ, NCOL], I32)
        last_idx = sb("last_idx", [NQ, NCOL], I32)
        has_edge = sb("has_edge", [NQ, NCOL])
        d1_idx = sb("d1_idx", [P, 1], I32)
        joined = sb("joined", [P, P])
        apart = sb("apart", [P, P])
        end_get = sb("end_get", [P, 1], I32)
        end_put = sb("end_put", [P, 1], I32)
        nf_d1 = sb("nf_d1", [P, C])
        m_spread = sb("m_spread", [P, H * P])
        jw = sb("jw", [P, H * P])
        jwT = sb("jwT", [P, H * P])
        m_in = sb("m_in", [P, H])
        m_end = sb("m_end", [P, H])
        m_all = sb("m_all", [P, H])
        j_exp = sb("j_exp", [P, 2, H])
        j_wts = sb("j_wts", [P, 2, H])
        u_end = sb("u_end", [P, HC])
        u_in = sb("u_in", [P, HC])
        rden = sb("rden", [NQ, NCOL * H])

        xT_ps = [ps(f"xT_ps{s}", [P, GT * P]) for s in range(2)]
        f_ps = [ps(f"f_ps{s}", [P, GT * P]) for s in range(2)]
        o_ps = [ps(f"o_ps{s}", [P, GT * P]) for s in range(2)]
        n_ps = ps("n_ps", [P, 2 * GT * P])

        z4 = U[0][0:NQ, 0:NCOL * HC].rearrange("q (b h c) -> q b h c", h=H, c=C)
        s4 = U[1][0:NQ, 0:NCOL * HD].rearrange("q (b h d) -> q b h d", h=H, d=D)

        dcol = U[0][:, 0:T + 1].bitcast(I32)
        dcolf = U[1][:, 0:T + 1]
        xmp = jw[:, 0:P].bitcast(I32)
        first_f, next_f, node_f, part_f = (rden[:, a * NCOL:(a + 1) * NCOL] for a in range(4))
        mean = m_spread[0:NQ, 0:NCOL]
        var = m_spread[0:NQ, NCOL:2 * NCOL]
        xc = ef_new[0][0:NQ, 0:NCOL * D].rearrange("q (b d) -> q b d", d=D)
        xsq = ef_new[1][0:NQ, 0:NCOL * D].rearrange("q (b d) -> q b d", d=D)
        x3 = x_sb[:, :].rearrange("q (b d) -> q b d", d=D)
        per = TB * K // T
        slots = ([rows[a][0:NQ, c * T:(c + 1) * T] for a in range(2) for c in range(per)]
                 + [U[1][0:NQ, T + 1 + c * T:T + 1 + (c + 1) * T]
                    for c in range((TB * HC - T - 1) // T)])
        assert len(slots) >= NCOL and NCOL % 5 == 0
        first3 = first_st[:, :].rearrange("p (t d) -> p t d", d=D)
        sc3 = [a[:, :].rearrange("p (t h) -> p t h", h=H) for a in sc]
        mx3 = [a[:, :].rearrange("p (t h) -> p t h", h=H) for a in mx]

        zeroed = sem("zeroed")
        made = sem("made")
        dst_in = sem("dst_in")
        src_in = sem("src_in")
        x_in = sem("x_in")
        prep = sem("prep")
        lasts_t = sem("lasts_t")
        rooted = sem("rooted")
        dst_out = sem("dst_out")
        chunk_idx = sem("chunk_idx")
        chunk_in = [sem(f"chunk_in{w}") for w in range(5)]
        counted = sem("counted")
        run_out = sem("run_out")
        run_in = sem("run_in")
        run_end_in = sem("run_end_in")
        nf_ready = sem("nf_ready")
        tab_out = sem("tab_out")
        w_in = sem("w_in")
        w_used = sem("w_used")
        first_out = sem("first_out")
        d1_in = sem("d1_in")
        idx_copied = sem("idx_copied")
        src_rows = [[sem(f"src_rows{s}_{a}") for a in range(7)] for s in range(2)]
        ef_in = sem("ef_in")
        first_in = sem("first_in")
        ef_spread = sem("ef_spread")
        dst_spread = sem("dst_spread")
        turned = sem("turned")
        xT_ready = sem("xT_ready")
        f_ready = sem("f_ready")
        f_low_ready = sem("f_low_ready")
        lr_ready = sem("lr_ready")
        o_ready = sem("o_ready")
        sc_ready = sem("sc_ready")
        ef_out = [sem(f"ef_out{s}") for s in range(2)]
        max_done = sem("max_done")
        expo_done = sem("expo_done")
        wts_ready = sem("wts_ready")
        prod_done = sem("prod_done")
        sums_done = sem("sums_done")
        u_out = [sem(f"u_out{s}") for s in range(2)]
        sliced = sem("sliced")
        normed = sem("normed")
        m_wide = sem("m_wide")
        m_turned = sem("m_turned")
        end_in = sem("end_in")
        j = sem("j")
        j_exp1 = sem("j_exp1")
        jw_turned = sem("jw_turned")
        u_in_ready = sem("u_in_ready")
        j_exp2 = sem("j_exp2")
        u_fixed = sem("u_fixed")
        z_in = [sem(f"z_in{a}") for a in range(3)]
        nd = sem("nd")
        s_turned = sem("s_turned")
        sT_ready = sem("sT_ready")
        n_ready = sem("n_ready")
        x_out = sem("x_out")

        passed = {e: sem(f"passed_{e}") for e in ("sp", "pool", "pe")}

        EFI = (48, 16)
        UI = (16 * NP, 16 * NP)
        DB = NQ
        AHEAD = 2
        HEAD = (NG + 1) // 2
        LEAKY_EVERY = 16

        def steps(i, span, last, turn, edges, scores):
            for jj in span:
                for stage, q in ((turn, jj + AHEAD), (edges, jj + 1), (scores, jj)):
                    for m in (2 * q, 2 * q + 1):
                        if m >= 0 and not (last and m >= 2 * NG):
                            stage(i + m // (2 * NG), m // NG % 2, m % NG)

        part_groups = [1, 2, 2, 3, 3, 3, NG - 14]
        part_of = [a for a, n in enumerate(part_groups) for _ in range(n)]
        groups = [range(g, min(g + GT, NCOL)) for g in range(0, NCOL, GT)]
        parts = [range(0, 2), range(2, 4), range(4, len(groups))]
        part_cols = [range(groups[p[0]][0], groups[p[-1]][-1] + 1) for p in parts]
        col_part = [a for a, cols in enumerate(part_cols) for _ in cols]
        NPART = len(parts)
        assert part_cols[2][0] * D == GT * P
        JS, NS = 11, 3 * NPART
        WAVES = 5
        WCOLS = NCOL // WAVES
        WI = 16 * (4 + 2 * H)

        with nc.Block() as block:

            @block.sync
            def _(eng):
                def store_nf():
                    eng.dma_start(nf_tab.rearrange("(q b) c -> q (b c)", b=NCOL), nf[:, :]
                                  ).then_inc(tab_out, 16)

                eng.wait_ge(zeroed, 3)
                eng.dma_start(dcol[0:FULL, 1:T + 1],
                              dst[0:FULL * T].rearrange("(p t) -> p t", t=T)).then_inc(dst_in, 16)
                eng.dma_start(dcol[FULL:FULL + 1, 1:REST + 1],
                              dst[FULL * T:E].rearrange("(p t) -> p t", p=1)).then_inc(dst_in, 16)
                eng.dma_start(dcol[1:FULL + 1, 0:1],
                              dst[T - 1:FULL * T].rearrange("(p t) -> p t", t=1)[::T, :]
                              , allow_slow_non_contiguous=True).then_inc(dst_in, 16)
                eng.dma_start(src_sb[0:FULL, :],
                              src[0:FULL * T].rearrange("(p t) -> p t", t=T)).then_inc(src_in, 16)
                eng.dma_start(src_sb[FULL:FULL + 1, 0:REST],
                              src[FULL * T:E].rearrange("(p t) -> p t", p=1)).then_inc(src_in, 16)
                eng.dma_start(x_sb[:, :],
                              x.rearrange("(q b) d -> q (b d)", b=NCOL)).then_inc(x_in, 16)
                eng.wait_ge(prep, 1)
                eng.dma_start(dst_tab[:, :], U[1][:, 1:T + 1]).then_inc(dst_out, 16)
                eng.wait_ge(nf_ready, NPART)
                store_nf()
                eng.wait_ge(prep, 12)
                eng.dma_start(run_tab[0:N, :].rearrange("(q b) o -> q (b o)", b=NCOL),
                              rden[:, 0:NCOL]).then_inc(run_out, 16)
                eng.dma_start(run_tab[N:N + 1, :], u_end[0:1, 0:1]).then_inc(run_out, 16)
                eng.wait_ge(run_out, 32)
                eng.dma_start(rden[:, NCOL:2 * NCOL],
                              run_tab[1:N + 1, :].rearrange("(q b) o -> q (b o)", b=NCOL)
                              ).then_inc(run_in, 16)

                with eng.Fori(0, L, 1) as l:
                    eng.wait_ge(w_used, l + 1)
                    eng.wait_ge(o_ready, l * (NB * NG) + 2)
                    eng.sem_inc(passed["sp"], 1)
                    lw = bass.ds(l, 1)

                    def one(ap):
                        return ap.rearrange("a b c -> (a b) c")
                    eng.dma_start(w_edge[0:D, :], one(W_ni[lw, :, :])).then_inc(w_in, 16)
                    eng.dma_start(w_edge[D:C, :], bias[lw, :]).then_inc(w_in, 16)
                    eng.dma_start(w_edge[DST0:EF0, :], one(W_nj[lw, :, :])).then_inc(w_in, 16)
                    eng.dma_start(w_edge[EF0:K, :], one(W_fij[lw, :, :])).then_inc(w_in, 16)
                    for h in range(H):
                        eng.dma_start(w_out[h * D:(h + 1) * D, h:h + 1],
                                      attn[lw, h, :].rearrange("a d -> d a"),
                                      allow_slow_non_contiguous=True).then_inc(w_in, 16)
                        eng.dma_start(w_node[h * D:(h + 1) * D, :],
                                      one(W_node[lw, :, h * D:(h + 1) * D])).then_inc(w_in, 16)
                    eng.wait_ge(ef_out[0], l * (16 * NP) + EFI[0])
                    eng.sem_inc(passed["sp"], 1)
                    eng.wait_ge(first_out, l * (16 * NCOL) + 16 * NCOL)
                    eng.sem_inc(passed["sp"], 1)

                    def load(k, b):
                        col = b * (TB * D)
                        eng.wait_ge(ef_spread, k + 1)
                        eng.dma_start(ef_st[:, :], ef_blk[:, bass.ds(col, TB * D)]
                                      ).then_inc(ef_in, 16)
                        eng.wait_ge(dst_spread, k * D + D)
                        eng.dma_start(first_st[:, :], first_blk[:, bass.ds(col, TB * D)]
                                      ).then_inc(first_in, 16)

                    def store(k, b, s):
                        eng.wait_ge(sums_done, k * HC + (l + (HC + 1)))
                        eng.dma_start(u_blk[:, bass.ds(b * (TB * HC), TB * HC)], U[s][:, :]
                                      ).then_inc(u_out[s], 16)
                        eng.dma_start(m_blk[:, bass.ds(b * (TB * H), TB * H)], mx[s][:, H:]
                                      ).then_inc(u_out[s], 16)

                    load(l * NB, 0)
                    eng.wait_ge(ef_out[1], l * (16 * NP) + EFI[1])
                    eng.sem_inc(passed["sp"], 1)
                    load(l * NB + 1, 1)
                    load(l * NB + 2, 2)
                    with eng.Fori(0, NP - 2, 1) as i:
                        for s in range(2):
                            b = i * 2 + s
                            load(l * NB + (b + 3), b + 3)
                            store(l * NB + b, b, s)
                    load(l * NB + (NB - 1), NB - 1)
                    for b in range(NB - 4, NB):
                        store(l * NB + b, b, b % 2)
                    eng.wait_ge(nf_ready, l * NPART + 2 * NPART)
                    store_nf()
                eng.wait_ge(nf_ready, (L + 1) * NPART + 1)
                eng.dma_start(out.rearrange("(q b) d -> q (b d)", b=NCOL), x_sb[:, :]
                              ).then_inc(x_out, 16)
                eng.wait_ge(x_out, 16)
                eng.wait_ge(tab_out, 16 * (L + 1))
                eng.wait_ge(ef_out[0], EFI[0] + 16 * NP * L)
                eng.wait_ge(ef_out[1], EFI[1] + 16 * NP * L)

            @block.gpsimd
            def _(eng):
                eng.iota(jw[:, 0:P].bitcast(I32), pattern=[[1, P]], base=0, channel_multiplier=-1
                         ).then_inc(made, 1)
                eng.iota(first_idx[:, :], pattern=[[1, NCOL]], base=0, channel_multiplier=NCOL
                         ).then_inc(made, 1)
                eng.iota(end_get[:, :], pattern=[[0, 1]], base=0, channel_multiplier=T
                         ).then_inc(made, 1)
                eng.wait_ge(dst_out, 16)
                eng.wait_ge(chunk_idx, 1)
                for b in range(NCOL):
                    eng.indirect_dma_start(slots[b], None, dst_tab[:, :],
                                           bass.IndirectOffsetOnAxis(
                                               ap=last_idx[:, b:b + 1], axis=0)
                                           ).then_inc(chunk_in[b // WCOLS], 16)
                eng.wait_ge(run_out, 32)
                eng.wait_ge(prep, 13)
                eng.indirect_dma_start(m_in[:, 0:1], None, run_tab[:, :],
                                       bass.IndirectOffsetOnAxis(ap=d1_idx[:, 0:1], axis=0)
                                       ).then_inc(run_end_in, 16)

                def waited():
                    eng.sem_inc(passed["pool"], 1)

                def scatter_first(l):
                    for b in range(NCOL):
                        if b == part_cols[col_part[b]][0]:
                            eng.wait_ge(nf_ready, l * NPART + (col_part[b] + 1))
                            waited()
                        eng.indirect_dma_start(edge_first[:, :],
                                               bass.IndirectOffsetOnAxis(
                                                   ap=first_idx[:, b:b + 1], axis=0),
                                               nf[:, b * C:b * C + D], None,
                                               bounds_check=P * T - 1, oob_is_err=False
                                               ).then_inc(first_out, 16)

                def gather_d1(l):
                    eng.wait_ge(tab_out, l * 16 + 16)
                    waited()
                    eng.indirect_dma_start(nf_d1[:, :], None, nf_tab[:, :],
                                           bass.IndirectOffsetOnAxis(ap=d1_idx[:, 0:1], axis=0)
                                           ).then_inc(d1_in, 16)

                def take_idx(l, i, s):
                    k = l * NB + i * 2 + s
                    eng.wait_ge(turned, k * NG + NG)
                    eng.wait_ge(prod_done, k + 1)
                    waited()
                    eng.tensor_copy(idx[s][:, :], src_sb[:, bass.ds((i * 2 + s) * TB, TB)]
                                    ).then_inc(idx_copied, 1)
                    eng.wait_ge(idx_copied, k + 1)
                    waited()

                def gather_cols(s, cols):
                    for t in cols:
                        eng.indirect_dma_start(rows[s][:, t * K:t * K + C], None, nf_tab[:, :],
                                               bass.IndirectOffsetOnAxis(
                                                   ap=idx[s][:, t:t + 1], axis=0)
                                               ).then_inc(src_rows[s][part_of[t // GT]], 16)

                def gather(l, i, s):
                    take_idx(l, i, s)
                    gather_cols(s, range(TB))

                def rest_of_layer(l):
                    with eng.Fori(0, NP - 1, 1) as i:
                        gather(l, i, 1)
                        gather(l, i + 1, 0)
                    gather(l, NP - 1, 1)
                    eng.wait_ge(u_out[0], l * (32 * NP) + (UI[0] + 32 * NP))
                    eng.wait_ge(u_out[1], l * (32 * NP) + (UI[1] + 32 * NP))
                    waited()
                    eng.indirect_dma_start(u_end[:, :], None, u_tab[:, :],
                                           bass.IndirectOffsetOnAxis(ap=end_get[:, 0:1], axis=0)
                                           ).then_inc(end_in, 16)
                    eng.indirect_dma_start(m_end[:, :], None, m_tab[:, :],
                                           bass.IndirectOffsetOnAxis(ap=end_get[:, 0:1], axis=0)
                                           ).then_inc(end_in, 16)
                    eng.wait_ge(j, l * JS + JS)
                    waited()
                    eng.indirect_dma_start(u_tab[:, :],
                                           bass.IndirectOffsetOnAxis(ap=end_put[:, 0:1], axis=0),
                                           u_end[:, :], None,
                                           bounds_check=P * T - 1, oob_is_err=False
                                           ).then_inc(u_fixed, 16)
                    eng.wait_ge(u_fixed, l * 16 + 16)
                    waited()
                    for b in range(NCOL):
                        eng.indirect_dma_start(U[0][0:NQ, b * HC:(b + 1) * HC], None,
                                               u_tab[:, :],
                                               bass.IndirectOffsetOnAxis(
                                                   ap=last_idx[:, b:b + 1], axis=0)
                                               ).then_inc(z_in[col_part[b]], 16)

                eng.wait_ge(counted, NCOL)
                eng.wait_ge(src_in, 32)
                eng.wait_ge(prep, 27)
                gather_d1(0)
                take_idx(0, 0, 0)
                gather_cols(0, range(TB // 2))
                eng.wait_ge(u_out[0], UI[0])
                eng.wait_ge(u_out[1], UI[1])
                scatter_first(0)
                gather_cols(0, range(TB // 2, TB))

                with eng.Fori(0, L - 1, 1) as l:
                    rest_of_layer(l)
                    scatter_first(l + 1)
                    gather_d1(l + 1)
                    gather(l + 1, 0, 0)
                rest_of_layer(L - 1)

            @block.tensor
            def _(eng):
                eng.wait_ge(prep, 3)
                eng.transpose(f_ps[0][:, 0:P], jwT[:, 0:P], ident[:, :]).then_inc(lasts_t, 1)
                eng.sem_inc(turned, 2 * NG)
                eng.sem_inc(f_ready, 2)
                eng.sem_inc(o_ready, 2)

                with eng.Fori(0, L, 1) as l:
                    eng.wait_ge(w_in, l * WI + WI)
                    eng.sem_inc(passed["pe"], 1)

                    def turn(i, s, g):
                        n, y = (l * NB + i * 2 + s) * NG + g, (s * NG + g) % 2
                        if g == 0:
                            k = l * NB + i * 2 + s
                            eng.wait_ge(dst_spread, k * D + 2 * D)
                            eng.wait_ge(ef_spread, k + 2)
                        a = part_of[g]
                        w = 16 * GT * part_groups[a]
                        if g == 0 or part_of[g - 1] != a:
                            eng.wait_ge(src_rows[s][a], (l * NP + i) * w + w)
                        eng.wait_ge(xT_ready, n + 1)
                        for u in range(GT):
                            mm = eng.transpose(xT_ps[y][0:K, u * P:(u + 1) * P],
                                               rows3[s][:, g * GT + u, :], ident[:, :])
                        mm.then_inc(turned, 1)

                    def edges(i, s, g):
                        n, y = (l * NB + i * 2 + s) * NG + g, (s * NG + g) % 2
                        eng.wait_ge(xT_ready, n + 3)
                        eng.wait_ge(lr_ready, n + 1)
                        eng.matmul(f_ps[y][:, :], w_edge[:, :], xT[y][0:K, :],
                                   start=True, stop=True).then_inc(f_ready, 1)

                    def scores(i, s, g):
                        n, y = (l * NB + i * 2 + s) * NG + g, (s * NG + g) % 2
                        eng.wait_ge(lr_ready, n + 3)
                        eng.wait_ge(sc_ready, n * 2 + 2)
                        for u in range(GT):
                            mm = eng.matmul(o_ps[y][:, u * M:(u + 1) * M],
                                            lr[y][:, u * P:(u + 1) * P], w_out[:, :],
                                            start=True, stop=True)
                        mm.then_inc(o_ready, 1)

                    steps(0, range(-AHEAD, 0), False, turn, edges, scores)
                    with eng.Fori(0, NP - 1, 1) as i:
                        steps(i, range(NG), False, turn, edges, scores)
                    steps(NP - 1, range(NG), True, turn, edges, scores)
                    eng.wait_ge(m_wide, l * H + H)
                    for h in range(H):
                        mm = eng.transpose(f_ps[0][:, h * P:(h + 1) * P],
                                           m_spread[:, h * P:(h + 1) * P], ident[:, :])
                    mm.then_inc(m_turned, 1)
                    eng.wait_ge(j, l * JS + 4)
                    for h in range(H):
                        mm = eng.transpose(f_ps[1][:, h * P:(h + 1) * P],
                                           jw[:, h * P:(h + 1) * P], ident[:, :])
                    mm.then_inc(jw_turned, 1)
                    eng.wait_ge(j, l * JS + 5)
                    for h in range(H):
                        mm = eng.matmul(o_ps[0][:, h * C:(h + 1) * C],
                                        jwT[:, h * P:(h + 1) * P],
                                        U3[1][:, TB - 1, h * C:(h + 1) * C],
                                        start=True, stop=True)
                    mm.then_inc(u_in_ready, 1)
                    def node_turn(n):
                        for a, p in enumerate(parts):
                            if n == p[0]:
                                eng.wait_ge(nd, l * NS + 3 * (a + 1))
                        if n >= 2:
                            eng.wait_ge(sT_ready, l * len(groups) + (n - 1))
                        for u, b in enumerate(groups[n]):
                            mm = eng.transpose(xT_ps[n % 2][:, u * DB:(u + 1) * DB],
                                               U[1][0:NQ, b * HD:(b + 1) * HD],
                                               ident[0:NQ, 0:NQ])
                        mm.then_inc(s_turned, 1)

                    for n in range(len(groups)):
                        if any(n == p[0] for p in parts):
                            node_turn(n)
                        if not any(n == p[-1] for p in parts):
                            node_turn(n + 1)
                        eng.wait_ge(sT_ready, l * len(groups) + (n + 1))
                        for u, b in enumerate(groups[n]):
                            mm = eng.matmul(n_ps[0:NQ, b * D:(b + 1) * D],
                                            xT[n % 2][:, u * DB:(u + 1) * DB], w_mean[:, :],
                                            start=True, stop=True)
                        mm.then_inc(n_ready, 1)

            @block.scalar
            def _(eng):
                eng.sem_inc(xT_ready, 2)
                eng.sem_inc(sc_ready, 4)
                eng.sem_inc(ef_spread, 1)
                eng.wait_ge(normed, 6)
                eng.activation(var, var, ACT.Sqrt).then_inc(rooted, 1)
                eng.wait_ge(run_in, 16)
                eng.wait_ge(run_end_in, 16)
                eng.wait_ge(zeroed, 5)
                for b in range(NB):
                    eng.dma_start(first_blk[:, b * TB * D:(b + 1) * TB * D], first_st[:, :]
                                  ).then_inc(u_out[b % 2], 16)
                eng.dma_start(ef_tab[E:P * T, :].rearrange("a d -> (a d)")
                              .rearrange("(r w) -> r w", r=PADR),
                              first_st[0:PADR, 0:PAD * D // PADR]).then_inc(ef_out[0], 16)
                eng.dma_start(ef_tab[FULL * T:E, :], edge_attr[FULL * T:E, :]
                              ).then_inc(ef_out[0], 16)
                attr_blk = edge_attr[0:FULL * T, :].rearrange("(p t) d -> p (t d)", t=T)
                for a, z in ((0, TB * D), (TB * D, T * D)):
                    eng.dma_start(ef_blk[0:FULL, a:z], attr_blk[:, a:z]
                                  ).then_inc(ef_out[1 if a else 0], 16)

                with eng.Fori(0, L, 1) as l:
                    def spread(k, s):
                        eng.wait_ge(ef_in, k * 16 + 16)
                        eng.wait_ge(turned, k * NG + NG)
                        eng.activation(rows3[s][:, :, EF0:K],
                                       ef_st[:, :].rearrange("p (t d) -> p t d", d=D),
                                       ACT.Copy).then_inc(ef_spread, 1)

                    def weigh(k):
                        eng.wait_ge(expo_done, k * 3 + 3)
                        eng.activation(wts[:, :, :], expo[:, :, :], ACT.Exp).then_inc(wts_ready, 1)

                    def take_xT(i, s, g, first):
                        if s == 0 and g == 4 and not first:
                            weigh(l * NB + i * 2 - 1)
                        n, y = (l * NB + i * 2 + s) * NG + g, (s * NG + g) % 2
                        eng.wait_ge(turned, n + 2 * NG + 1)
                        eng.wait_ge(f_ready, n + 1)
                        eng.activation(xT[y][0:K, :], xT_ps[y][0:K, :], ACT.Copy
                                       ).then_inc(xT_ready, 1)

                    def lower(i, s, g):
                        n, y = (l * NB + i * 2 + s) * NG + g, (s * NG + g) % 2
                        eng.wait_ge(f_ready, n + 3)
                        eng.wait_ge(lr_ready, n + 1)
                        eng.activation(f_low[y][:, :], f_ps[y][:, :], ACT.Copy, scale=SLOPE
                                       ).then_inc(f_low_ready, 1)

                    def take_scores(i, s, g, last):
                        k = l * NB + i * 2 + s
                        n, y = k * NG + g, (s * NG + g) % 2
                        if g == 0:
                            eng.wait_ge(prod_done, k + 1)
                            eng.wait_ge(ef_out[s], (l * NP + i) * 16 + EFI[s])
                        eng.wait_ge(o_ready, n + 3)
                        o3 = o_ps[y][:, 0:GT * M].rearrange("p (t m) -> p t m", m=M)
                        eng.activation(sc[s][:, g * GT * H:(g + 1) * GT * H]
                                       .rearrange("p (t h) -> p t h", h=H),
                                       o3[:, :, 0:H], ACT.Copy).then_inc(sc_ready, 1)
                        eng.activation(ef_new[s][:, g * GT * D:(g + 1) * GT * D]
                                       .rearrange("p (t d) -> p t d", d=D),
                                       o3[:, :, H:M], ACT.Copy).then_inc(sc_ready, 1)
                        if s == 1 and g == 0:
                            weigh(k - 1)
                        if g == NG // 3 and not (last and s == 1):
                            spread(k + 1, 1 - s)
                        if g == NG - 1:
                            eng.wait_ge(sc_ready, k * (2 * NG) + (2 * NG + 4))
                            eng.dma_start(ef_blk[:, bass.ds((i * 2 + s) * (TB * D), TB * D)],
                                          ef_new[s][:, :]).then_inc(ef_out[s], 16)

                    spread(l * NB, 0)
                    steps(0, range(-AHEAD, HEAD), False,
                          lambda i, s, g: take_xT(i, s, g, s == 0), lower,
                          lambda i, s, g: take_scores(i, s, g, False))
                    with eng.Fori(0, NP - 1, 1) as i:
                        steps(i, range(HEAD, NG + HEAD), False,
                              lambda i, s, g: take_xT(i, s, g, False), lower,
                              lambda i, s, g: take_scores(i, s, g, False))
                    steps(NP - 1, range(HEAD, NG), True,
                          lambda i, s, g: take_xT(i, s, g, False), lower,
                          lambda i, s, g: take_scores(i, s, g, True))
                    weigh(l * NB + (NB - 1))

                    eng.wait_ge(j, l * JS + 3)
                    eng.activation(jw[:, :], jw[:, :], ACT.Exp).then_inc(j_exp1, 1)
                    eng.wait_ge(j, l * JS + 8)
                    eng.activation(j_wts[:, :, :], j_exp[:, :, :], ACT.Exp).then_inc(j_exp2, 1)
                    for n in range(len(groups)):
                        w = len(groups[n]) * DB
                        eng.wait_ge(s_turned, l * len(groups) + (n + 1))
                        if n >= 2:
                            eng.wait_ge(n_ready, l * len(groups) + (n - 1))
                        eng.activation(xT[n % 2][:, 0:w], xT_ps[n % 2][:, 0:w], ACT.Copy
                                       ).then_inc(sT_ready, 1)

            @block.vector
            def _(eng):
                def wide(ap, shape):
                    return ap.broadcast_to(shape)

                eng.memset(dcol, N).then_inc(zeroed, 1)
                eng.memset(src_sb[:, :], 0).then_inc(zeroed, 1)
                eng.wait_ge(zeroed, 2)
                eng.memset(dcol[0:1, 0:1], -1).then_inc(zeroed, 1)
                eng.memset(u_end[:, :], float(E)).then_inc(zeroed, 1)
                eng.memset(first_st[:, :], 0.0).then_inc(zeroed, 1)
                eng.sem_inc(lr_ready, 2)
                eng.sem_inc(prod_done, 2)
                eng.sem_inc(dst_spread, D)
                eng.wait_ge(dst_in, 48)
                eng.tensor_copy(dcolf, dcol).then_inc(prep, 1)
                eng.wait_ge(made, 3)
                eng.tensor_scalar(ident[:, :], xmp, 0.0, None, ALU.is_equal).then_inc(prep, 1)
                eng.wait_ge(prep, 1)
                eng.tensor_copy(jwT[:, 0:P], wide(dcolf[:, T:T + 1], [P, P])).then_inc(prep, 1)
                eng.tensor_tensor(same[:, :], dcolf[:, 1:T + 1], dcolf[:, 0:T], ALU.is_equal
                                  ).then_inc(prep, 1)
                eng.wait_ge(prep, 4)
                eng.tensor_scalar(cut[:, :], same[:, :], -1.0, BIG, ALU.add, ALU.mult
                                  ).then_inc(prep, 1)
                eng.tensor_copy(node_f, first_idx[:, :]).then_inc(prep, 1)
                eng.wait_ge(prep, 6)
                eng.wait_ge(lasts_t, 1)
                below = U[0][0:NQ, 0:NCOL * P].rearrange("q (b p) -> q b p", p=P)
                eng.tensor_tensor(below,
                                  wide(f_ps[0][0:NQ, 0:P].rearrange("q (o p) -> q o p", o=1),
                                       [NQ, NCOL, P]),
                                  wide(node_f.rearrange("q (b o) -> q b o", o=1), [NQ, NCOL, P]),
                                  ALU.is_lt).then_inc(prep, 1)
                eng.wait_ge(prep, 7)
                eng.tensor_reduce(part_f, below, AX.X, ALU.add).then_inc(prep, 1)
                eng.wait_ge(prep, 8)
                eng.tensor_copy(last_idx[:, :], part_f).then_inc(chunk_idx, 1)
                eng.tensor_scalar(jwT[:, P:2 * P], xmp, 0.0, None, ALU.is_lt).then_inc(prep, 1)
                eng.wait_ge(prep, 9)
                eng.scalar_tensor_tensor(joined[:, :], f_ps[0][:, 0:P], dcolf[:, 1:2],
                                         jwT[:, P:2 * P], ALU.is_equal, ALU.mult
                                         ).then_inc(prep, 1)
                eng.wait_ge(prep, 10)
                eng.tensor_scalar(apart[:, :], joined[:, :], -1.0, BIG, ALU.add, ALU.mult
                                  ).then_inc(prep, 1)
                eng.wait_ge(x_in, 16)
                wide_q = [NQ, NCOL, D]
                eng.tensor_reduce(mean, x3, AX.X, ALU.add).then_inc(normed, 1)
                eng.wait_ge(normed, 1)
                eng.tensor_scalar(mean, mean, 1.0 / D, None, ALU.mult).then_inc(normed, 1)
                eng.wait_ge(normed, 2)
                mean_w = wide(mean.rearrange("q (b o) -> q b o", o=1), wide_q)
                var_w = wide(var.rearrange("q (b o) -> q b o", o=1), wide_q)
                eng.tensor_tensor(xc, x3, mean_w, ALU.subtract).then_inc(normed, 1)
                eng.wait_ge(normed, 3)
                eng.tensor_tensor(xsq, xc, xc, ALU.mult).then_inc(normed, 1)
                eng.wait_ge(normed, 4)
                eng.tensor_reduce(var, xsq, AX.X, ALU.add).then_inc(normed, 1)
                eng.wait_ge(normed, 5)
                eng.tensor_scalar(var, var, 1.0 / D, 1e-5, ALU.mult, ALU.add).then_inc(normed, 1)
                eng.wait_ge(rooted, 1)
                eng.reciprocal(var, var).then_inc(normed, 1)
                eng.wait_ge(normed, 7)
                eng.tensor_tensor(xc, xc, var_w, ALU.mult).then_inc(normed, 1)
                eng.wait_ge(normed, 8)
                eng.memset(nf3[:, :, D:C], 1.0)
                eng.tensor_scalar(nf3[:, :, 0:D], xc, 0.0, None, ALU.max).then_inc(nf_ready, NPART)
                eng.memset(w_out[:, :], 0.0).then_inc(normed, 1)
                eng.wait_ge(normed, 9)
                eng.tensor_reduce(w_out[:, H:M], ident[:, :].rearrange("p (h d) -> p d h", d=D),
                                  AX.X, ALU.add).then_inc(normed, 1)
                eng.wait_ge(normed, 10)
                eng.tensor_scalar(w_out[:, H:M], w_out[:, H:M], 1.0 / H, None, ALU.mult
                                  ).then_inc(w_used, 1)
                for b in range(NCOL):
                    if b % WCOLS == 0:
                        eng.wait_ge(chunk_in[b // WCOLS], 16 * WCOLS)
                    o = b % (TB * HC // T)
                    if b > o:
                        eng.wait_ge(counted, b - TB * HC // T + 1)
                    eng.tensor_scalar(U[0][0:NQ, o * T:(o + 1) * T],
                                      slots[b], node_f[:, b:b + 1], None,
                                      ALU.is_lt, ALU.add, accum_out=first_f[:, b:b + 1]
                                      ).then_inc(counted, 1)
                eng.wait_ge(counted, NCOL)
                eng.scalar_tensor_tensor(first_f, part_f, float(T), first_f, ALU.mult, ALU.add
                                         ).then_inc(prep, 1)
                eng.tensor_scalar(d1_idx[:, :], dcolf[:, 1:2], 1.0, float(N), ALU.add, ALU.min
                                  ).then_inc(prep, 1)
                eng.tensor_copy(m_in[:, 1:2], end_get[:, :]).then_inc(prep, 1)
                eng.tensor_scalar(m_in[:, 2:3], dcolf[:, 1:2], float(N - 1), None, ALU.min
                                  ).then_inc(prep, 1)
                eng.wait_ge(run_in, 16)
                eng.wait_ge(run_end_in, 16)
                eng.tensor_tensor(has_edge[:, :], first_f, next_f, ALU.is_lt).then_inc(prep, 1)
                eng.wait_ge(prep, 16)
                eng.scalar_tensor_tensor(last_idx[:, :], next_f, -1.0, has_edge[:, :],
                                         ALU.add, ALU.mult).then_inc(prep, 1)
                eng.tensor_scalar(part_f, has_edge[:, :], -FAR, FAR, ALU.mult, ALU.add
                                  ).then_inc(prep, 1)
                eng.wait_ge(prep, 18)
                eng.tensor_tensor(first_idx[:, :], part_f, first_f, ALU.add).then_inc(prep, 1)
                col, here = m_end[:, 0:1], m_end[:, 1:2]
                eng.scalar_tensor_tensor(col, m_in[:, 0:1], -1.0, m_in[:, 1:2],
                                         ALU.add, ALU.subtract).then_inc(prep, 1)
                eng.wait_ge(prep, 20)
                eng.tensor_scalar(here, col, 0.0, None, ALU.is_ge).then_inc(prep, 1)
                eng.wait_ge(prep, 21)
                eng.scalar_tensor_tensor(here, col, float(T), here, ALU.is_lt, ALU.mult
                                         ).then_inc(prep, 1)
                eng.wait_ge(prep, 22)
                eng.tensor_tensor(m_end[:, 2:3], col, here, ALU.mult).then_inc(prep, 1)
                eng.tensor_scalar(m_end[:, 3:4], here, -FAR, FAR, ALU.mult, ALU.add
                                  ).then_inc(prep, 1)
                eng.wait_ge(prep, 24)
                eng.tensor_tensor(end_get[:, :], m_in[:, 1:2], m_end[:, 2:3], ALU.add
                                  ).then_inc(prep, 1)
                eng.scalar_tensor_tensor(end_put[:, :], m_in[:, 0:1], -1.0, m_end[:, 3:4],
                                         ALU.add, ALU.add).then_inc(prep, 1)
                eng.tensor_copy(d1_idx[:, :], m_in[:, 2:3]).then_inc(prep, 1)
                eng.wait_ge(prep, 27)

                with eng.Fori(0, L, 1) as l:
                    eng.wait_ge(w_in, l * WI + WI)
                    eng.tensor_scalar(w_mean[:, :], w_node[:, :], 1.0 / H, None, ALU.mult
                                      ).then_inc(w_used, 1)
                    eng.memset(U3[1][:, TB - 1, :], 0.0).then_inc(sums_done, 1)
                    eng.memset(mx3[1][:, TB, :], -BIG).then_inc(max_done, 1)

                    def slice_b(k, col, s):
                        eng.tensor_copy(same_b[s][:, :], same[:, bass.ds(col, TB)]
                                        ).then_inc(sliced, 1)
                        eng.tensor_copy(cut_b[s][:, :], cut[:, bass.ds(col, TB)]
                                        ).then_inc(sliced, 1)

                    def spread_dst(k, s, first):
                        eng.wait_ge(first_in, k * 16 + 16)
                        eng.wait_ge(turned, k * NG + NG)
                        eng.wait_ge(sliced, k * 2 + 2)
                        eng.wait_ge(dst_spread, k * D + D)
                        for d in range(D):
                            before = (nf_d1[:, d:d + 1] if first
                                      else rows3[1 - s][:, TB - 1, DST0 + d:DST0 + d + 1])
                            eng.tensor_tensor_scan(rows3[s][:, :, DST0 + d], same_b[s][:, :],
                                                   first3[:, :, d], before,
                                                   ALU.mult, ALU.add).then_inc(dst_spread, 1)

                    def leaky2(n):
                        for y in range(2):
                            eng.wait_ge(f_low_ready, n + (y + 1))
                            eng.wait_ge(o_ready, n + (y + 1))
                            eng.tensor_tensor(lr[y][:, :], f_ps[y][:, :], f_low[y][:, :], ALU.max
                                              ).then_inc(lr_ready, 1)

                    def recur(k, i, s, more, spread):
                        eng.wait_ge(sc_ready, k * (2 * NG) + (2 * NG + 4))
                        eng.wait_ge(u_out[s], (l * NP + i) * 32 + UI[s])
                        eng.wait_ge(max_done, k * (H + 1) + (l + 1))
                        eng.tensor_copy(mx3[s][:, 0, :], mx3[1 - s][:, TB, :]
                                        ).then_inc(max_done, 1)
                        for h in range(H):
                            eng.tensor_tensor_scan(mx3[s][:, 1:TB + 1, h], cut_b[s][:, :],
                                                   sc3[s][:, :, h], mx3[1 - s][:, TB, h:h + 1],
                                                   ALU.add, ALU.max).then_inc(max_done, 1)
                        eng.wait_ge(max_done, k * (H + 1) + (l + (H + 2)))
                        ex = [expo[:, a, :].rearrange("p (t h) -> p t h", h=H) for a in range(2)]
                        eng.tensor_tensor(ex[0], mx3[s][:, 0:TB, :], mx3[s][:, 1:TB + 1, :],
                                          ALU.subtract).then_inc(expo_done, 1)
                        eng.tensor_tensor(ex[1], sc3[s], mx3[s][:, 1:TB + 1, :],
                                          ALU.subtract).then_inc(expo_done, 1)
                        eng.wait_ge(expo_done, k * 3 + 2)
                        eng.tensor_tensor(ex[0], ex[0],
                                          wide(cut_b[s][:, :].rearrange("p (t o) -> p t o", o=1),
                                               [P, TB, H]), ALU.add).then_inc(expo_done, 1)
                        twos = [(k + 1) * NG + g for g in range(1 - s, NG, 2)] if more else []

                        def next_leaky():
                            if twos:
                                leaky2(twos.pop(0))

                        next_leaky()
                        eng.wait_ge(wts_ready, k + 1)
                        tbh = [P, TB, H, C]
                        eng.tensor_tensor(
                            U3[s].rearrange("p t (h c) -> p t h c", c=C),
                            wide(rows3[s][:, :, 0:C].rearrange("p t (o c) -> p t o c", o=1), tbh),
                            wide(wts[:, 1, :].rearrange("p (t h o) -> p t h o", h=H, o=1), tbh),
                            ALU.mult).then_inc(prod_done, 1)
                        if spread:
                            next_leaky()
                            slice_b(k + 2, (i * 2 + (s + 2)) * TB, s)
                            spread_dst(k + 2, s, False)
                            next_leaky()
                        eng.wait_ge(prod_done, k + 3)
                        eng.wait_ge(sums_done, k * HC + (l + 1))
                        decay = wts[:, 0, :].rearrange("p (t h) -> p t h", h=H)
                        for c in range(HC):
                            eng.tensor_tensor_scan(U3[s][:, :, c], decay[:, :, c // C],
                                                   U3[s][:, :, c], U3[1 - s][:, TB - 1, c:c + 1],
                                                   ALU.mult, ALU.add).then_inc(sums_done, 1)
                            if c % LEAKY_EVERY == LEAKY_EVERY - 1:
                                next_leaky()

                    eng.wait_ge(d1_in, l * 16 + 16)
                    for s in range(2):
                        slice_b(l * NB + s, s * TB, s)
                        spread_dst(l * NB + s, s, s == 0)
                        for g in range(6 * s, NG + 1 if s else 6, 2):
                            leaky2(l * NB * NG + g)
                    with eng.Fori(0, NP - 1, 1) as i:
                        for s in range(2):
                            recur(l * NB + i * 2 + s, i, s, True, True)
                    recur(l * NB + (NB - 2), NP - 1, 0, True, False)
                    recur(l * NB + (NB - 1), NP - 1, 1, False, False)

                    for h in range(H):
                        eng.tensor_copy(m_spread[:, h * P:(h + 1) * P],
                                        wide(mx3[1][:, TB, h:h + 1], [P, P])
                                        ).then_inc(m_wide, 1)
                    hpp = [P, H, P]
                    jw3 = jw[:, :].rearrange("p (h q) -> p h q", h=H)
                    eng.wait_ge(m_turned, l + 1)
                    eng.tensor_tensor(jw3, f_ps[0][:, :].rearrange("p (h q) -> p h q", h=H),
                                      wide(apart[:, :].rearrange("p (o q) -> p o q", o=1), hpp),
                                      ALU.add).then_inc(j, 1)
                    eng.wait_ge(j, l * JS + 1)
                    eng.tensor_reduce(m_in[:, :], jw3, AX.X, ALU.max).then_inc(j, 1)
                    eng.wait_ge(j, l * JS + 2)
                    eng.tensor_tensor(jw3, jw3,
                                      wide(m_in[:, :].rearrange("p (h o) -> p h o", o=1), hpp),
                                      ALU.subtract).then_inc(j, 1)
                    eng.wait_ge(j_exp1, l + 1)
                    eng.tensor_tensor(jw3, jw3,
                                      wide(joined[:, :].rearrange("p (o q) -> p o q", o=1), hpp),
                                      ALU.mult).then_inc(j, 1)
                    eng.wait_ge(jw_turned, l + 1)
                    eng.tensor_copy(jwT[:, :], f_ps[1][:, :]).then_inc(j, 1)
                    eng.wait_ge(end_in, l * 32 + 32)
                    eng.tensor_tensor(m_all[:, :], m_in[:, :], m_end[:, :], ALU.max
                                      ).then_inc(j, 1)
                    eng.wait_ge(j, l * JS + 6)
                    eng.tensor_tensor(j_exp[:, 0, :], m_in[:, :], m_all[:, :], ALU.subtract
                                      ).then_inc(j, 1)
                    eng.tensor_tensor(j_exp[:, 1, :], m_end[:, :], m_all[:, :], ALU.subtract
                                      ).then_inc(j, 1)
                    eng.wait_ge(j_exp2, l + 1)
                    eng.wait_ge(u_in_ready, l + 1)
                    phc = [P, H, C]
                    w_j = [wide(j_wts[:, a, :].rearrange("p (h o) -> p h o", o=1), phc)
                           for a in range(2)]
                    u_in3 = u_in[:, :].rearrange("p (h c) -> p h c", h=H)
                    u_end3 = u_end[:, :].rearrange("p (h c) -> p h c", h=H)
                    eng.tensor_tensor(u_in3, o_ps[0][:, 0:HC].rearrange("p (h c) -> p h c", h=H),
                                      w_j[0], ALU.mult).then_inc(j, 1)
                    eng.tensor_tensor(u_end3, u_end3, w_j[1], ALU.mult).then_inc(j, 1)
                    eng.wait_ge(j, l * JS + 10)
                    eng.tensor_tensor(u_end[:, :], u_end[:, :], u_in[:, :], ALU.add
                                      ).then_inc(j, 1)

                    rden3 = rden[:, :].rearrange("q (b h) -> q b h", h=H)
                    for a, cols in enumerate(part_cols):
                        c, n = slice(cols[0], cols[-1] + 1), len(cols)
                        eng.wait_ge(z_in[a], l * (16 * n) + 16 * n)
                        eng.reciprocal(rden3[:, c, :], z4[:, c, :, D]).then_inc(nd, 1)
                        eng.wait_ge(nd, l * NS + (3 * a + 1))
                        eng.tensor_tensor(rden3[:, c, :], rden3[:, c, :],
                                          wide(has_edge[:, c].rearrange("q (b o) -> q b o", o=1),
                                               [NQ, n, H]), ALU.mult).then_inc(nd, 1)
                        eng.wait_ge(nd, l * NS + (3 * a + 2))
                        eng.tensor_tensor(s4[:, c, :, :], z4[:, c, :, 0:D],
                                          wide(rden3[:, c, :]
                                               .rearrange("q b (h o) -> q b h o", o=1),
                                               [NQ, n, H, D]), ALU.mult).then_inc(nd, 1)
                        eng.wait_ge(n_ready, l * len(groups) + (parts[a][-1] + 1))
                        eng.tensor_copy(nf3[:, c, 0:D],
                                        n_ps[0:NQ, c.start * D:c.stop * D]
                                        .rearrange("q (b d) -> q b d", d=D)
                                        ).then_inc(nf_ready, 1)
                eng.wait_ge(nf_ready, (L + 1) * NPART)
                eng.tensor_tensor(x3, x3, nf3[:, :, 0:D], ALU.add).then_inc(nf_ready, 1)


_INS = ['x', 'src', 'dst', 'edge_attr_32', 'L0_gnn_W_ni', 'L0_gnn_W_nj', 'L0_gnn_W_fij',
        'L0_gnn_W_node', 'L0_gnn_attn', 'L0_gnn_bias']


def kernel(**inputs):
    import numpy as _np
    import concourse.bacc as _bacc
    from concourse import mybir as _mybir
    from concourse.bass_utils import run_bass_kernel_spmd as _run

    nc = _bacc.Bacc("TRN2", target_bir_lowering=False, num_devices=1)
    arrays, args = {}, []
    for name in _INS:
        a = _np.ascontiguousarray(inputs[name])
        arrays[f"in_{name}_dram"] = a
        args.append(nc.dram_tensor(f"in_{name}_dram", a.shape, _mybir.dt.from_np(a.dtype),
                                   kind="ExternalInput").ap())
    args.append(nc.dram_tensor("out_0_dram", inputs['x'].shape, _mybir.dt.float32,
                               kind="ExternalOutput").ap())
    egat_kernel(nc, *args)
    r = _run(nc, [arrays], core_ids=[0])
    return r.results[0]["out_0_dram"]
```
